# Optimizing a Trainium2 kernel written in Bass

```python
import numpy as np
import jax
import jax.numpy as jnp

def _softmax(x, axis=-1):
    return jax.nn.softmax(x, axis=axis)

def _gelu(x):
    return jax.nn.gelu(x, approximate=True)

def _silu(x):
    return jax.nn.silu(x)

def _sigmoid(x):
    return jax.nn.sigmoid(x)

def _layernorm(x, axis=-1, eps=1e-05):
    m = jnp.mean(x, axis=axis, keepdims=True)
    v = jnp.var(x, axis=axis, keepdims=True)
    return (x - m) / jnp.sqrt(v + eps)

def _scatter_add(tgt, idx, src, axis=0):
    return tgt.at[idx].add(src)

def _segment_sum(src, seg, n):
    return jax.ops.segment_sum(src, seg, n)
kernel_name = 'mk_xattn_seq_d2_seqx_r8_897d04'

def setup_inputs(seed: int=0):
    np.random.seed(seed)
    _w = jnp.asarray

    def _rec_inputs():
        import jax
        import jax.numpy as jnp
        _rk = jax.random.key(seed)
        x = -0.0002928 + 1 * jax.random.normal(jax.random.fold_in(_rk, 1), (64, 64, 256), jnp.float32)
        _lenS = 64 - jax.random.randint(jax.random.fold_in(_rk, 7), (64,), 0, max(1, 64 // 4) + 1, jnp.int32)
        _lenS2 = 64 - jax.random.randint(jax.random.fold_in(_rk, 8), (64,), 0, max(1, 64 // 4) + 1, jnp.int32)
        _ctx_2048P = jax.random.normal(jax.random.fold_in(_rk, 11), (64, 16, 256), jnp.float32)
        _ctx_2048c = jax.random.dirichlet(jax.random.fold_in(_rk, 511), 0.3 * jnp.ones((16,), jnp.float32), (64, 64))
        _ctx_2048t = jnp.einsum('bsk,bkd->bsd', _ctx_2048c, _ctx_2048P)
        _ctx_2048t = _ctx_2048t * jax.lax.rsqrt(jnp.mean(jnp.square(_ctx_2048t)) + 1e-12) * 0.953939
        ctx_2048 = -1.39393e-06 + 0.999914 * (_ctx_2048t + 0.3 * jax.random.normal(jax.random.fold_in(_rk, 611), (64, 64, 256), jnp.float32))
        _validS = jnp.arange(64)[None, :] < _lenS[:, None]
        _validS2 = jnp.arange(64)[None, :] < _lenS2[:, None]
        _causal = jnp.tril(jnp.ones((64, 64), dtype=bool))
        mask_1x1xSxS2_fc1 = jnp.where(jnp.broadcast_to(_validS2[0:1, None, None, :], (1, 1, 64, 64)), 1.0, 0.0).astype(jnp.float32)
        mask_Bx1xSxS2_ff1 = jnp.where(jnp.ones((64, 1, 64, 64), dtype=bool), 1.0, 0.0).astype(jnp.float32)
        mask_BxS2_bf1 = jnp.ones((64, 64), dtype=bool)
        return (x, ctx_2048, mask_1x1xSxS2_fc1, mask_Bx1xSxS2_ff1, mask_BxS2_bf1)
    x, ctx_2048, mask_1x1xSxS2_fc1, mask_Bx1xSxS2_ff1, mask_BxS2_bf1 = _rec_inputs()

    def _L0_xattn_setup():
        import jax, jax.numpy as jnp
        import numpy as np
        H = 256
        NH = 16
        HD = H // NH
        EPS = 1e-05

        def gelu(x):
            return 0.5 * x * (1.0 + jnp.tanh(0.7978845608028654 * x * (1.0 + 0.044715 * x * x)))

        def layernorm(x, scale, bias):
            m = jnp.mean(x, axis=-1, keepdims=True)
            v = jnp.mean(jnp.square(x - m), axis=-1, keepdims=True)
            return (x - m) * jax.lax.rsqrt(v + EPS) * scale + bias

        def split_heads(x):
            b, s, _ = x.shape
            return x.reshape(b, s, NH, HD).transpose(0, 2, 1, 3)

        def merge_heads(x):
            b, nh, s, hd = x.shape
            return x.transpose(0, 2, 1, 3).reshape(b, s, nh * hd)

        def attention(q, k, v, mask):
            scores = jnp.einsum('bhqd,bhkd->bhqk', q, k) / jnp.sqrt(jnp.float32(HD))
            scores = scores * mask - 10000.0 * (1.0 - mask)
            probs = jax.nn.softmax(scores, axis=-1)
            return jnp.einsum('bhqk,bhkd->bhqd', probs, v)
        key = jax.random.key(seed)
        ks = jax.random.split(key, 16)
        b, s, t = (2, 128, 128)
        w = lambda k, i, o: jax.random.normal(k, (i, o), jnp.float32) * 0.02
        inp = {'hidden_states': jax.random.normal(ks[0], (b, s, H), jnp.float32), 'encoder_states': jax.random.normal(ks[1], (b, t, H), jnp.float32), 'ltor_mask': jnp.tril(jnp.ones((1, 1, s, s), jnp.float32)), 'cross_mask': jnp.ones((b, 1, s, t), jnp.float32), 'ln1_s': jnp.ones((H,), jnp.float32), 'ln1_b': jnp.zeros((H,), jnp.float32), 'w_qkv': w(ks[2], H, 3 * H), 'b_qkv': jnp.zeros((3 * H,), jnp.float32), 'w_ao': w(ks[3], H, H), 'b_ao': jnp.zeros((H,), jnp.float32), 'ln2_s': jnp.ones((H,), jnp.float32), 'ln2_b': jnp.zeros((H,), jnp.float32), 'w_q': w(ks[4], H, H), 'b_q': jnp.zeros((H,), jnp.float32), 'w_kv': w(ks[5], H, 2 * H), 'b_kv': jnp.zeros((2 * H,), jnp.float32), 'w_co': w(ks[6], H, H), 'b_co': jnp.zeros((H,), jnp.float32), 'ln3_s': jnp.ones((H,), jnp.float32), 'ln3_b': jnp.zeros((H,), jnp.float32), 'w1': w(ks[7], H, 4 * H), 'b1': jnp.zeros((4 * H,), jnp.float32), 'w2': w(ks[8], 4 * H, H), 'b2': jnp.zeros((H,), jnp.float32)}
        return inp
    _L0_xattn_all = _L0_xattn_setup()
    _L0_xattn_in = {k: v for k, v in _L0_xattn_all.items() if k in ('ln1_s', 'ln1_b', 'w_qkv', 'b_qkv', 'w_ao', 'b_ao', 'ln2_s', 'ln2_b', 'w_q', 'b_q', 'w_kv', 'b_kv', 'w_co', 'b_co', 'ln3_s', 'ln3_b', 'w1', 'b1', 'w2', 'b2')}
    del _L0_xattn_all

    def _L1_xattn_setup():
        import jax, jax.numpy as jnp
        import numpy as np
        HIDDEN = 256
        HEADS = 16
        HEAD_DIM = HIDDEN // HEADS
        LN_EPS = 1e-05
        GATE_INIT = 0.5

        def _layer_norm(x, gamma, beta):
            mu = jnp.mean(x, axis=-1, keepdims=True)
            var = jnp.mean(jnp.square(x - mu), axis=-1, keepdims=True)
            return (x - mu) * jax.lax.rsqrt(var + LN_EPS) * gamma + beta
        key = jax.random.key(seed)
        ks = jax.random.split(key, 8)
        B, T_TEXT, T_AUDIO = (4, 256, 1500)
        s = 0.02
        return {'hidden_states': jax.random.normal(ks[0], (B, T_TEXT, HIDDEN), jnp.float32), 'audio_kv': jax.random.normal(ks[1], (B, T_AUDIO, HIDDEN), jnp.float32), 'audio_attention_mask': jnp.ones((B, T_AUDIO), dtype=bool), 'Wq': jax.random.normal(ks[2], (HIDDEN, HIDDEN), jnp.float32) * s, 'Wk': jax.random.normal(ks[3], (HIDDEN, HIDDEN), jnp.float32) * s, 'Wv': jax.random.normal(ks[4], (HIDDEN, HIDDEN), jnp.float32) * s, 'Wo': jax.random.normal(ks[5], (HIDDEN, HIDDEN), jnp.float32) * s, 'ln_gamma': jnp.ones((HIDDEN,), jnp.float32), 'ln_beta': jnp.zeros((HIDDEN,), jnp.float32), 'gate': jnp.array([GATE_INIT], jnp.float32)}
    _L1_xattn_all = _L1_xattn_setup()
    _L1_xattn_in = {k: v for k, v in _L1_xattn_all.items() if k in ('Wq', 'Wk', 'Wv', 'Wo', 'ln_gamma', 'ln_beta', 'gate')}
    del _L1_xattn_all
    return {'x': x, 'ctx_2048': ctx_2048, 'mask_1x1xSxS2_fc1': mask_1x1xSxS2_fc1, 'mask_Bx1xSxS2_ff1': mask_Bx1xSxS2_ff1, 'mask_BxS2_bf1': mask_BxS2_bf1, 'L0_xattn_ln1_s': _L0_xattn_in['ln1_s'], 'L0_xattn_ln1_b': _L0_xattn_in['ln1_b'], 'L0_xattn_w_qkv': _L0_xattn_in['w_qkv'], 'L0_xattn_b_qkv': _L0_xattn_in['b_qkv'], 'L0_xattn_w_ao': _L0_xattn_in['w_ao'], 'L0_xattn_b_ao': _L0_xattn_in['b_ao'], 'L0_xattn_ln2_s': _L0_xattn_in['ln2_s'], 'L0_xattn_ln2_b': _L0_xattn_in['ln2_b'], 'L0_xattn_w_q': _L0_xattn_in['w_q'], 'L0_xattn_b_q': _L0_xattn_in['b_q'], 'L0_xattn_w_kv': _L0_xattn_in['w_kv'], 'L0_xattn_b_kv': _L0_xattn_in['b_kv'], 'L0_xattn_w_co': _L0_xattn_in['w_co'], 'L0_xattn_b_co': _L0_xattn_in['b_co'], 'L0_xattn_ln3_s': _L0_xattn_in['ln3_s'], 'L0_xattn_ln3_b': _L0_xattn_in['ln3_b'], 'L0_xattn_w1': _L0_xattn_in['w1'], 'L0_xattn_b1': _L0_xattn_in['b1'], 'L0_xattn_w2': _L0_xattn_in['w2'], 'L0_xattn_b2': _L0_xattn_in['b2'], 'L1_xattn_Wq': _L1_xattn_in['Wq'], 'L1_xattn_Wk': _L1_xattn_in['Wk'], 'L1_xattn_Wv': _L1_xattn_in['Wv'], 'L1_xattn_Wo': _L1_xattn_in['Wo'], 'L1_xattn_ln_gamma': _L1_xattn_in['ln_gamma'], 'L1_xattn_ln_beta': _L1_xattn_in['ln_beta'], 'L1_xattn_gate': _L1_xattn_in['gate']}

def reference(x, ctx_2048, mask_1x1xSxS2_fc1, mask_Bx1xSxS2_ff1, mask_BxS2_bf1, L0_xattn_ln1_s, L0_xattn_ln1_b, L0_xattn_w_qkv, L0_xattn_b_qkv, L0_xattn_w_ao, L0_xattn_b_ao, L0_xattn_ln2_s, L0_xattn_ln2_b, L0_xattn_w_q, L0_xattn_b_q, L0_xattn_w_kv, L0_xattn_b_kv, L0_xattn_w_co, L0_xattn_b_co, L0_xattn_ln3_s, L0_xattn_ln3_b, L0_xattn_w1, L0_xattn_b1, L0_xattn_w2, L0_xattn_b2, L1_xattn_Wq, L1_xattn_Wk, L1_xattn_Wv, L1_xattn_Wo, L1_xattn_ln_gamma, L1_xattn_ln_beta, L1_xattn_gate):
    import jax
    import jax.numpy as jnp

    def _L0_xattn_ref(hidden_states, encoder_states, ltor_mask, cross_mask, ln1_s, ln1_b, w_qkv, b_qkv, w_ao, b_ao, ln2_s, ln2_b, w_q, b_q, w_kv, b_kv, w_co, b_co, ln3_s, ln3_b, w1, b1, w2, b2):
        import jax, jax.numpy as jnp
        import numpy as np
        H = 256
        NH = 16
        HD = H // NH
        EPS = 1e-05

        def gelu(x):
            return 0.5 * x * (1.0 + jnp.tanh(0.7978845608028654 * x * (1.0 + 0.044715 * x * x)))

        def layernorm(x, scale, bias):
            m = jnp.mean(x, axis=-1, keepdims=True)
            v = jnp.mean(jnp.square(x - m), axis=-1, keepdims=True)
            return (x - m) * jax.lax.rsqrt(v + EPS) * scale + bias

        def split_heads(x):
            b, s, _ = x.shape
            return x.reshape(b, s, NH, HD).transpose(0, 2, 1, 3)

        def merge_heads(x):
            b, nh, s, hd = x.shape
            return x.transpose(0, 2, 1, 3).reshape(b, s, nh * hd)

        def attention(q, k, v, mask):
            scores = jnp.einsum('bhqd,bhkd->bhqk', q, k) / jnp.sqrt(jnp.float32(HD))
            scores = scores * mask - 10000.0 * (1.0 - mask)
            probs = jax.nn.softmax(scores, axis=-1)
            return jnp.einsum('bhqk,bhkd->bhqd', probs, v)
        ln_out = layernorm(hidden_states, ln1_s, ln1_b)
        qkv = ln_out @ w_qkv + b_qkv
        q, k, v = jnp.split(qkv, 3, axis=-1)
        ctx = merge_heads(attention(split_heads(q), split_heads(k), split_heads(v), ltor_mask))
        attn_out = ctx @ w_ao + b_ao
        x = hidden_states + attn_out
        ln_out = layernorm(x, ln2_s, ln2_b)
        q = ln_out @ w_q + b_q
        kv = encoder_states @ w_kv + b_kv
        k, v = jnp.split(kv, 2, axis=-1)
        ctx = merge_heads(attention(split_heads(q), split_heads(k), split_heads(v), cross_mask))
        cross_out = ctx @ w_co + b_co
        x = x + cross_out
        ln_out = layernorm(x, ln3_s, ln3_b)
        mlp_out = gelu(ln_out @ w1 + b1) @ w2 + b2
        return x + mlp_out

    def _L1_xattn_ref(hidden_states, audio_kv, audio_attention_mask, Wq, Wk, Wv, Wo, ln_gamma, ln_beta, gate):
        import jax, jax.numpy as jnp
        import numpy as np
        HIDDEN = 256
        HEADS = 16
        HEAD_DIM = HIDDEN // HEADS
        LN_EPS = 1e-05
        GATE_INIT = 0.5

        def _layer_norm(x, gamma, beta):
            mu = jnp.mean(x, axis=-1, keepdims=True)
            var = jnp.mean(jnp.square(x - mu), axis=-1, keepdims=True)
            return (x - mu) * jax.lax.rsqrt(var + LN_EPS) * gamma + beta
        B, Tt, D = hidden_states.shape
        Ta = audio_kv.shape[1]
        scale = HEAD_DIM ** (-0.5)
        a = _layer_norm(audio_kv, ln_gamma, ln_beta)
        Q = (hidden_states @ Wq.T).reshape(B, Tt, HEADS, HEAD_DIM).transpose(0, 2, 1, 3)
        K = (a @ Wk.T).reshape(B, Ta, HEADS, HEAD_DIM).transpose(0, 2, 1, 3)
        V = (a @ Wv.T).reshape(B, Ta, HEADS, HEAD_DIM).transpose(0, 2, 1, 3)
        scores = jnp.einsum('bhtd,bhsd->bhts', Q, K) * scale
        mask = audio_attention_mask[:, None, None, :]
        scores = jnp.where(mask, scores, jnp.float32(-jnp.inf))
        attn = jax.nn.softmax(scores, axis=-1)
        out = jnp.einsum('bhts,bhsd->bhtd', attn, V)
        out = out.transpose(0, 2, 1, 3).reshape(B, Tt, D)
        out = out @ Wo.T
        return hidden_states + jnp.tanh(gate) * out
    x = _L0_xattn_ref(x, ctx_2048, mask_1x1xSxS2_fc1, mask_Bx1xSxS2_ff1, L0_xattn_ln1_s, L0_xattn_ln1_b, L0_xattn_w_qkv, L0_xattn_b_qkv, L0_xattn_w_ao, L0_xattn_b_ao, L0_xattn_ln2_s, L0_xattn_ln2_b, L0_xattn_w_q, L0_xattn_b_q, L0_xattn_w_kv, L0_xattn_b_kv, L0_xattn_w_co, L0_xattn_b_co, L0_xattn_ln3_s, L0_xattn_ln3_b, L0_xattn_w1, L0_xattn_b1, L0_xattn_w2, L0_xattn_b2)
    x = _L1_xattn_ref(x, ctx_2048, mask_BxS2_bf1, L1_xattn_Wq, L1_xattn_Wk, L1_xattn_Wv, L1_xattn_Wo, L1_xattn_ln_gamma, L1_xattn_ln_beta, L1_xattn_gate)
    return x

_drawn_inputs = setup_inputs


def setup_inputs(seed=0):
    import zlib

    import numpy as np

    out = dict(_drawn_inputs(seed))
    spreads = {'L0_xattn_ln1_s': (1.0, 0.6),
     'L0_xattn_ln1_b': (0.0, 0.766),
     'L0_xattn_b_qkv': (0.0, 0.272),
     'L0_xattn_b_ao': (0.0, 0.1),
     'L0_xattn_ln2_s': (1.0, 0.6),
     'L0_xattn_ln2_b': (0.0, 2.0),
     'L0_xattn_b_q': (0.0, 2.0),
     'L0_xattn_b_kv': (0.0, 0.283),
     'L0_xattn_b_co': (0.0, 0.1),
     'L0_xattn_ln3_s': (1.0, 0.6),
     'L0_xattn_ln3_b': (0.0, 0.655),
     'L0_xattn_b1': (0.0, 0.1),
     'L0_xattn_b2': (0.0, 0.1),
     'L1_xattn_ln_gamma': (1.0, 0.6),
     'L1_xattn_ln_beta': (0.0, 0.8)}
    factors = {'L0_xattn_w_qkv': 3.124, 'L0_xattn_w_q': 8.0, 'L1_xattn_Wq': 8.0, 'L1_xattn_Wk': 8.0}
    for name, (base, spread) in spreads.items():
        noise = np.random.default_rng([zlib.crc32(name.encode()), seed]).standard_normal(out[name].shape)
        drawn = base * np.exp(spread * noise) if base else spread * noise
        out[name] = jnp.asarray(drawn.astype(out[name].dtype))
    for name, factor in factors.items():
        out[name] = (out[name] * factor).astype(out[name].dtype)
    return out
```

```python
from contextlib import ExitStack

import concourse.bass as bass
from concourse import mybir

F32 = mybir.dt.float32
F32R = mybir.dt.float32r
U8 = mybir.dt.uint8
ALU = mybir.AluOpType
ACT = mybir.ActivationFunctionType
AX = mybir.AxisListType

NB, S, H = 64, 64, 256
NH = 16
HD = H // NH
FF = 4 * H
P = 128
TILE = P // S
T = 2
UB = T * TILE
TOK = UB * S
U = NB // UB
KC = H // P
R = 4
C2 = NH // 2 // R
VW = 2 * HD + 1
BANK = 512
EPS = 1e-5
OFF = 10000.0
FAR = 1e30

STAGES = "PABMC"
LAG = {s: n for n, s in enumerate(STAGES)}
FIRST = len(STAGES)
TAIL = len(STAGES) - 1
PJ = ["C.xT", "C.zT", "C.Q", "C.K", "C.V", "B.zT", "B.cT", "B.Q", "B.K", "B.V", "M.zT", "C.OT",
      "M.H0", "M.H1", "C.AO", "M.H2", "M.H3", "A.zT", "A.Q", "A.K", "A.V", "B.OT", "M.Y", "B.AO",
      "A.OT", "A.AO"]
ATT = "CBA"
GELU = 4


def unit(stage, i):
    return i - LAG[stage]


def active(stage, i):
    return not isinstance(i, int) or 0 <= unit(stage, i) < U


def pj_bank(name):
    return PJ.index(name) % 2


def pj_use(name, i):
    k, b = PJ.index(name), pj_bank(name)
    if isinstance(i, int):
        return sum(active(n[0], j) for j in range(i) for n in PJ[b::2]) + sum(
            active(n[0], i) for n in PJ[b:k + 1:2])
    return pj_use(name, FIRST) + (i - FIRST) * len(PJ[b::2])


def before(a, i):
    if not isinstance(i, int):
        n = ATT.index(a)
        return (ATT[n - 1], unit(ATT[n - 1], i) + 1) if n else (ATT[-1], unit(ATT[-1], i))
    done = [(x, unit(x, j) + 1) for j in range(i) for x in ATT if active(x, j)]
    done += [(x, unit(x, i) + 1) for x in ATT[:ATT.index(a)] if active(x, i)]
    return done[-1] if done else None


def build(nc, d, out):
    ctx = ExitStack()
    with ctx:
        def sb(name, shape, dt=F32):
            return ctx.enter_context(nc.sbuf_tensor(name, shape, dt))

        def ps(name):
            return ctx.enter_context(nc.psum_tensor(name, [P, BANK], F32))

        def sem(name):
            return ctx.enter_context(nc.semaphore(name))

        WCOLS = {"A_qkv": (3 * H, KC), "A_o": (H, KC), "B_q": (H, KC), "B_kv": (2 * H, KC),
                 "B_o": (H, KC), "M_1": (FF, KC), "M_2": (H, FF // P), "C_q": (H, KC),
                 "C_k": (H, KC), "C_v": (H, KC), "C_o": (H, KC)}
        w_hi = {n: sb(f"w_hi_{n}", [P, k, c], F32R) for n, (c, k) in WCOLS.items()}
        w_lo = {n: sb(f"w_lo_{n}", [P, k, c], F32R) for n, (c, k) in WCOLS.items()}

        ident = sb("ident", [P, P])
        parity = sb("parity", [P, 2])
        qscale = sb("qscale", [P, 2])
        lnvec = sb("lnvec", [P, 4, 2, KC])
        NBIAS, BC, BB = 24, 16, 20
        bias_in = sb("bias_in", [P, NBIAS])
        bias = sb("bias", [P, NBIAS])
        BQ, BK, BV, BH = {"A": 0, "B": 6}, {"A": 2, "B": 20, "C": 16}, {"A": 4, "B": 22, "C": 18}, 8
        qbias = sb("qbias", [P, 2, 2, KC])
        brow = sb("brow", [P, 3, H])
        gate = sb("gate", [P, 1])
        gate_t = sb("gate_t", [P, 1])
        half = sb("half", [P, T])
        eps = sb("eps", [P, T])
        maskA = sb("maskA", [P, TILE, S])
        maskA_off = sb("maskA_off", [P, TILE, S])

        x_in = sb("x_in", [P, T, H])
        ctx_b = sb("ctx_b", [P, T, H])
        ctx_c = sb("ctx_c", [P, T, H])
        z = {"A": sb("z_A", [P, T, H]), "B": sb("z_B", [P, T, H]), "M": sb("z_M", [P, T, H]),
             "C": ctx_c}
        xb = {s: sb(f"xb_{s}", [P, T, H]) for s in "ABM"}
        x12 = sb("x12", [P, T, H])
        x3 = sb("x3", [P, T, H])
        y = sb("y", [P, T, H])
        stats = sb("stats", [P, 4, T, 6])
        mv = sb("mv", [P, 4, T, 2])
        veps = sb("veps", [P, 4, T])
        rstd = sb("rstd", [P, 4, T])
        maskB = sb("maskB", [P, UB, S])
        maskB_off = sb("maskB_off", [P, UB, S])
        maskC = sb("maskC", [P, UB, S], U8)
        maskC_off = sb("maskC_off", [P, UB, S])
        op = {k: (sb(f"{k}_hi", [P, KC, TOK], F32R), sb(f"{k}_lo", [P, KC, TOK], F32R))
              for k in ("zT_AC", "zT_B", "xT_C_cT_B", "zT_M", "oT")}
        OP = {"A.zT": op["zT_AC"], "C.zT": op["zT_AC"], "B.zT": op["zT_B"],
              "B.cT": op["xT_C_cT_B"], "C.xT": op["xT_C_cT_B"], "M.zT": op["zT_M"],
              "A.OT": op["oT"], "B.OT": op["oT"], "C.OT": op["oT"]}
        q2 = {a: sb(f"q2_{a}", [P, KC, UB, 2, S]) for a in "ABC"}
        kT = {a: sb(f"kT_{a}", [P, KC, TOK]) for a in "ABC"}
        vz = {a: sb(f"vz_{a}", [P, T, R * C2, TILE, VW]) for a in "ABC"}
        prob = {"B": sb("prob_B", [P, R, T * C2, TILE * S]),
                "A": sb("prob_AC", [P, R, T * C2, TILE * S])}
        prob["C"] = prob["A"]
        rmax = {a: sb(f"rmax_{a}", [P, R, T * C2 * TILE]) for a in "ABC"}
        rden = {a: sb(f"rden_{a}", [P, R, T * C2 * TILE]) for a in "ABC"}
        o = sb("o", [P, UB, 2, R, C2 * HD])
        g = sb("g", [P, 2, 2, TOK])
        h_hi = sb("h_hi", [P, FF // P, TOK], F32R)
        h_lo = sb("h_lo", [P, FF // P, TOK], F32R)

        s_bank = [ps(f"s_bank{r}") for r in range(R)]
        pv_bank = [ps(f"pv_bank{n}") for n in range(2)]
        pj = [ps(f"pj{n}") for n in range(2)]

        const_in = sem("const_in")
        stage_in = [sem(f"stage_in{n}") for n in range(6)]
        setup_pe, setup_scaled, setup_hi, setup_lo = (sem(f"setup_{n}") for n in ("pe", "scaled", "hi", "lo"))
        bias_done, gate_done, masks_done = sem("bias_done"), sem("gate_done"), sem("masks_done")
        setup_pool = sem("setup_pool")
        half_set, zeroed = sem("half_set"), sem("zeroed")
        x_in_s, ctxb_s, ctxc_s, maskb_s, maskc_s = (sem(n) for n in ("x_in_s", "ctxb_s", "ctxc_s", "maskb_s", "maskc_s"))
        pj_full = [sem(f"pj_full{n}") for n in range(2)]
        pj_free = [sem(f"pj_free{n}") for n in range(2)]
        hi_done = {n: sem("hi_" + n.replace(".", "_")) for n in OP}
        scored = {a: sem(f"scored_{a}") for a in "ABC"}
        masked = {a: sem(f"masked_{a}") for a in "ABC"}
        offset = {a: sem(f"offset_{a}") for a in "AB"}
        maxed = {a: sem(f"maxed_{a}") for a in "ABC"}
        shifted = {a: sem(f"shifted_{a}") for a in "ABC"}
        exped = {a: sem(f"exped_{a}") for a in "ABC"}
        turned = {a: sem(f"turned_{a}") for a in "ABC"}
        turned_in = {a: sem(f"turned_in_{a}") for a in "ABC"}
        summed = {a: sem(f"summed_{a}") for a in "ABC"}
        inverted = {a: sem(f"inverted_{a}") for a in "ABC"}
        normed = {a: sem(f"normed_{a}") for a in "ABC"}
        gelued, h_hi_done, h_lo_done = sem("gelued"), sem("h_hi_done"), sem("h_lo_done")
        tokens = {s: sem(f"tokens_{s}") for s in "ABMC"}
        ln_stats = {s: sem(f"ln_stats_{s}") for s in "ABMC"}
        ln_mv = {s: sem(f"ln_mv_{s}") for s in "ABMC"}
        ln_eps = {s: sem(f"ln_eps_{s}") for s in "ABMC"}
        ln_rstd = {s: sem(f"ln_rstd_{s}") for s in "ABMC"}
        ln_done = {s: sem(f"ln_done_{s}") for s in "ABMC"}
        xb_done = {s: sem(f"xb_done_{s}") for s in "ABM"}
        maskb_off_s, maskc_off_s = sem("maskb_off_s"), sem("maskc_off_s")
        stored = sem("stored")

        LN = {"A": 0, "B": 1, "M": 2, "C": 3}

        x_d = d["x"].rearrange("(u t b) s c -> u (b s) t c", t=T, b=TILE)
        c_d = d["ctx_2048"].rearrange("(u t b) s c -> u (b s) t c", t=T, b=TILE)
        y_d = out.rearrange("(u t b) s c -> u (b s) t c", t=T, b=TILE)
        mB_d = d["mask_Bx1xSxS2_ff1"].rearrange("(u b) o q k -> u (o q) b k", b=UB)
        mC_d = d["mask_BxS2_bf1"].rearrange("(u o b) k -> u o (b k)", b=UB, o=1)

        def rows(name):
            return d[name].rearrange("(k p) c -> p k c", p=P)

        stage_buf = [prob["A"], prob["B"]]

        def staged(slot, at, k, c):
            flat = stage_buf[slot][:, :, :, :].rearrange("p a b c -> p (a b c)")
            return flat[:, at:at + k * c].rearrange("p (k c) -> p k c", k=k)

        GROUPS = [[("A_qkv", "A")],
                  [("A_o", None), ("B_q", "B"), ("B_o", None), ("C_q", None)],
                  [("B_kv", None), ("C_k", "C"), ("C_v", "C")],
                  [("M_1", "M")],
                  [("M_2", None)],
                  [("C_o", "gate")]]
        pieces = []
        for n, group in enumerate(GROUPS):
            at = 0
            for name, scaled in group:
                c, k = WCOLS[name]
                pieces.append((n, name, scaled, staged(n % 2, at, k, c), k))
                at += k * c
            assert at <= R * T * C2 * TILE * S
        last_piece = [max(m for m, p in enumerate(pieces) if p[0] == n) for n in range(len(GROUPS))]
        N_CONST = 0

        block = ctx.enter_context(nc.Block())

        FEATURE = {"A.Q": ("A.zT", "A_qkv", 0), "A.K": ("A.zT", "A_qkv", H),
                   "B.Q": ("B.zT", "B_q", 0), "B.K": ("B.cT", "B_kv", 0),
                   "C.Q": ("C.xT", "C_q", 0), "C.K": ("C.zT", "C_k", 0),
                   **{f"M.H{m}": ("M.zT", "M_1", m * 2 * P) for m in range(GELU)}}
        TOKEN = {"A.V": ("A.zT", "A_qkv", 2 * H), "B.V": ("B.cT", "B_kv", H), "C.V": ("C.zT", "C_v", 0),
                 "A.AO": ("A.OT", "A_o", 0), "B.AO": ("B.OT", "B_o", 0), "C.AO": ("C.OT", "C_o", 0)}

        def run(eng, body, first, last):
            for i in range(first, min(FIRST, last + 1)):
                body(i)
            with eng.Fori(FIRST, U) as i:
                body(i)
            for i in range(U, last + 1):
                body(i)

        LAST = U - 1 + TAIL

        @block.sync
        def _(sp):
            n = [0]

            def const(dst, src):
                sp.dma_start(dst, src).then_inc(const_in, 16)
                n[0] += 16

            def load_group(k):
                for m, name, scaled, dst, kc in pieces:
                    if m == k:
                        sp.dma_start(dst, rows("w_" + name)).then_inc(stage_in[k], 16)

            def value(x):
                return x if isinstance(x, int) else sp.snap(x)

            def tokens_in(i):
                if active("P", i):
                    u = unit("P", i)
                    if not isinstance(i, int) or u:
                        sp.wait_ge(ln_done["A"], u)
                        sp.wait_ge(xb_done["A"], u)
                    sp.dma_start(x_in[:, :, :], x_d[i]).then_inc(x_in_s, 16)

            load_group(0)
            const(ident[:, :], d["identity"])
            const(parity[:, :], d["parity"])
            const(lnvec[:, :, :, :].rearrange("p n v k -> p (n v k)"), d["ln_vectors"])
            const(bias_in[:, 0:BC], d["biases"][:, 0:BC])
            const(bias_in[:, BB:NBIAS], d["biases"][:, BC:])
            for k, v in enumerate(("L0_xattn_b_ao", "L0_xattn_b_co", "L0_xattn_b2")):
                const(brow[:, k, :], d[v].rearrange("(o c) -> o c", o=1).broadcast_to([P, H]))
            const(gate[:, :], d["L1_xattn_gate"].rearrange("(o c) -> o c", o=1).broadcast_to([P, 1]))
            for half_p in range(2):
                for b in range(TILE):
                    const(maskA[half_p * S:(half_p + 1) * S, b, :], d["mask_1x1xSxS2_fc1"][0, 0])
            assert n[0] == CONST
            load_group(1)
            for k in range(2, len(GROUPS)):
                sp.wait_ge(setup_lo, last_piece[k - 2] + 1)
                load_group(k)

            def body(i):
                later = not isinstance(i, int)
                b_turned = value(pj_use("B.cT", i - 1)) if later or active("B", i - 1) else 0
                b_masked = value(R * unit("B", i))
                u_b, u_m, c_out = value(unit("B", i)), value(unit("M", i)), value(unit("C", i) + 1)
                c_turned = value(pj_use("C.zT", i))
                tokens_in(i)
                if active("B", i):
                    u = u_b
                    if later or u:
                        sp.wait_ge(pj_full[pj_bank("B.cT")], b_turned)
                    sp.dma_start(ctx_b[:, :, :], c_d[u]).then_inc(ctxb_s, 16)
                    if later or u:
                        sp.wait_ge(masked["B"], b_masked)
                        sp.wait_ge(maskb_off_s, u)
                    for hp in range(2):
                        sp.dma_start(maskB[hp * S:(hp + 1) * S, :, :], mB_d[u]).then_inc(maskb_s, 16)
                if active("M", i):
                    u = u_m
                    if later or u:
                        sp.wait_ge(maskc_off_s, u)
                        sp.wait_ge(pj_full[pj_bank("C.zT")], c_turned)
                    sp.dma_start(ctx_c[:, :, :], c_d[u]).then_inc(ctxc_s, 16)
                    sp.dma_start(maskC[:, :, :].rearrange("p b k -> p (b k)"),
                                 mC_d[u].broadcast_to([P, UB * S])).then_inc(maskc_s, 16)
                if active("C", i):
                    sp.wait_ge(tokens["C"], c_out)
                    sp.dma_start(y_d[unit("C", i)], y[:, :, :]).then_inc(stored, 16)

            run(sp, body, 0, LAST)
            sp.wait_ge(stored, 16 * U)

        @block.tensor
        def _(pe):
            pe.wait_ge(const_in, CONST)
            pe.wait_ge(setup_pool, 1)
            first = True
            for n, (group, name, scaled, w, kc) in enumerate(pieces):
                if scaled not in ("A", "B", "M", "C"):
                    continue
                pe.wait_ge(stage_in[group], 16 * len(GROUPS[group]))
                shift = lnvec[:, LN[scaled], 1, :]
                cols = WCOLS[name][0]
                at = {"A_qkv": 0, "B_q": 6, "M_1": 8, "C_k": 16, "C_v": 18}[name]
                for m in range(cols // P):
                    is_v = name == "C_v" or (name == "A_qkv" and m >= 4)
                    for k in range(KC):
                        if is_v:
                            lhs = w[:, k, cols - H + m % 2 * P:cols - H + (m % 2 + 1) * P]
                        else:
                            lhs = w[:, k, m * P:(m + 1) * P]
                        last = nc.tensor.matmul(pj[0][:, at + m:at + m + 1], lhs, shift[:, k:k + 1],
                                                start=(k == 0), stop=(k == KC - 1))
                last.then_inc(setup_pe, 1)

            pe.wait_ge(setup_lo, len(pieces))
            pe.wait_ge(bias_done, 1)

            def claim(name, i):
                n = pj_use(name, i) - 1
                if not isinstance(n, int) or n:
                    pe.wait_ge(pj_free[pj_bank(name)], n)
                return pj[pj_bank(name)]

            def turn(name, src, i):
                bank = claim(name, i)
                for k in range(KC):
                    for t in range(T):
                        at = k * TOK + t * P
                        last = nc.tensor.transpose(bank[:, at:at + P], src[:, t, k * P:(k + 1) * P], ident[:, :])
                last.then_inc(pj_full[pj_bank(name)], 1)

            def parts(x, w):
                return ((x[0], w_hi[w]), (x[1], w_hi[w]), (x[0], w_lo[w]))

            def feature_major(name, i):
                src, w, col = FEATURE[name]
                pe.wait_ge(pj_free[pj_bank(src)], pj_use(src, i))
                bank = claim(name, i)
                for m in range(2):
                    n = 0
                    for k in range(KC):
                        for x, wt in parts(OP[src], w):
                            last = nc.tensor.matmul(bank[:, m * TOK:(m + 1) * TOK],
                                                    wt[:, k, col + m * P:col + (m + 1) * P], x[:, k, :],
                                                    start=(n == 0), stop=(n == 3 * KC - 1))
                            n += 1
                last.then_inc(pj_full[pj_bank(name)], 1)

            def token_major(name, i):
                src, w, col = TOKEN[name]
                pe.wait_ge(pj_free[pj_bank(src)], pj_use(src, i))
                bank = claim(name, i)
                for t in range(T):
                    n = 0
                    for k in range(KC):
                        for x, wt in parts(OP[src], w):
                            last = nc.tensor.matmul(bank[:, t * H:(t + 1) * H], x[:, k, t * P:(t + 1) * P],
                                                    wt[:, k, col:col + H],
                                                    start=(n == 0), stop=(n == 3 * KC - 1))
                            n += 1
                last.then_inc(pj_full[pj_bank(name)], 1)

            def mlp_out(i):
                u = unit("M", i)
                pe.wait_ge(h_lo_done, GELU * (u + 1))
                bank = claim("M.Y", i)
                for t in range(T):
                    n = 0
                    for k in range(FF // P):
                        for x, wt in ((h_hi, w_hi["M_2"]), (h_lo, w_hi["M_2"]), (h_hi, w_lo["M_2"])):
                            last = nc.tensor.matmul(bank[:, t * H:(t + 1) * H], x[:, k, t * P:(t + 1) * P],
                                                    wt[:, k, :], start=(n == 0), stop=(n == 3 * (FF // P) - 1))
                            n += 1
                last.then_inc(pj_full[pj_bank("M.Y")], 1)

            def scores(a, i):
                u = unit(a, i)
                for name in (f"{a}.Q", f"{a}.K"):
                    pe.wait_ge(pj_free[pj_bank(name)], pj_use(name, i))
                if b := before(a, i):
                    pe.wait_ge(turned_in[b[0]], R * b[1])
                for t in range(T):
                    for c in range(C2):
                        for b2 in range(TILE):
                            tok = (t * TILE + b2) * S
                            at = ((t * C2 + c) * TILE + b2) * S
                            for r in range(R):
                                g32 = slice(32 * r, 32 * r + 32)
                                mm = nc.tensor.matmul(s_bank[r][:, at:at + S],
                                                      q2[a][g32, c, t * TILE + b2].rearrange("p e q -> p (e q)"),
                                                      kT[a][g32, c, tok:tok + S], start=True, stop=True)
                                if (t, c, b2) == (T - 1, C2 - 1, TILE - 1):
                                    mm.then_inc(scored[a], 1)

            def turn_probs(a, r, i):
                pe.wait_ge(exped[a], R * unit(a, i) + r + 1)
                for n in range(T * C2):
                    last = nc.tensor.transpose(s_bank[r][:, n * P:(n + 1) * P], prob[a][:, r, n, :], ident[:, :])
                last.then_inc(turned[a], 1)

            def values(a, r, i):
                u = unit(a, i)
                if r == 0:
                    pe.wait_ge(pj_free[pj_bank(f"{a}.V")], pj_use(f"{a}.V", i))
                pe.wait_ge(turned_in[a], R * u + r + 1)
                if r >= 2:
                    pe.wait_ge(normed[a], R * u + r - 1)
                elif b := before(a, i):
                    pe.wait_ge(normed[b[0]], R * b[1])
                pv = pv_bank[r % 2][:, 0:UB * C2 * VW].rearrange("p (t b c v) -> p t c b v", t=T, b=TILE, c=C2)
                for t in range(T):
                    for c in range(C2):
                        last = nc.tensor.matmul(pv[:, t, c], prob[a][:, r, t * C2 + c, :],
                                                vz[a][:, t, r * C2 + c, :, :], start=True, stop=True)
                last.then_inc(summed[a], 1)

            def attend(a, i):
                for r in range(R):
                    turn_probs(a, r, i)
                for r in range(R):
                    values(a, r, i)

            def turn_out(a, i):
                name = f"{a}.OT"
                pe.wait_ge(normed[a], R * (unit(a, i) + 1))
                bank = claim(name, i)
                for e in range(2):
                    for t in range(T):
                        for b2 in range(TILE):
                            at = e * TOK + (t * TILE + b2) * S
                            last = nc.tensor.matmul(bank[:, at:at + S],
                                                    o[:, t * TILE + b2, e].rearrange("p r f -> p (r f)"),
                                                    ident[:, e * S:(e + 1) * S], start=True, stop=True)
                last.then_inc(pj_full[pj_bank(name)], 1)

            def body(i):
                if active("C", i):
                    u = unit("C", i)
                    pe.wait_ge(tokens["M"], u + 1)
                    turn("C.xT", x3, i)
                    pe.wait_ge(ln_done["C"], u + 1)
                    turn("C.zT", ctx_c, i)
                    feature_major("C.Q", i)
                    feature_major("C.K", i)
                    token_major("C.V", i)
                    scores("C", i)
                if active("B", i):
                    u = unit("B", i)
                    pe.wait_ge(ln_done["B"], u + 1)
                    turn("B.zT", z["B"], i)
                    pe.wait_ge(ctxb_s, 16 * (u + 1))
                    turn("B.cT", ctx_b, i)
                    feature_major("B.Q", i)
                    feature_major("B.K", i)
                    token_major("B.V", i)
                if active("M", i):
                    pe.wait_ge(ln_done["M"], unit("M", i) + 1)
                    turn("M.zT", z["M"], i)
                if active("C", i):
                    attend("C", i)
                if active("B", i):
                    scores("B", i)
                if active("C", i):
                    turn_out("C", i)
                if active("M", i):
                    feature_major("M.H0", i)
                    feature_major("M.H1", i)
                if active("C", i):
                    token_major("C.AO", i)
                if active("M", i):
                    feature_major("M.H2", i)
                    feature_major("M.H3", i)
                if active("B", i):
                    attend("B", i)
                if active("A", i):
                    pe.wait_ge(ln_done["A"], unit("A", i) + 1)
                    turn("A.zT", z["A"], i)
                    feature_major("A.Q", i)
                    feature_major("A.K", i)
                    token_major("A.V", i)
                    scores("A", i)
                if active("B", i):
                    turn_out("B", i)
                if active("M", i):
                    mlp_out(i)
                if active("B", i):
                    token_major("B.AO", i)
                if active("A", i):
                    attend("A", i)
                    turn_out("A", i)
                    token_major("A.AO", i)

            run(pe, body, 1, LAST)

        @block.scalar
        def _(act):
            act.wait_ge(const_in, CONST)
            nc.scalar.activation(gate_t[:, :], gate[:, :], ACT.Tanh).then_inc(gate_done, 1)
            for n, (group, name, scaled, w, kc) in enumerate(pieces):
                act.wait_ge(stage_in[group], 16 * len(GROUPS[group]))
                if scaled:
                    act.wait_ge(setup_scaled, sum(bool(p[2]) for p in pieces[:n + 1]))
                nc.scalar.activation(w_hi[name][:, :, :], w, ACT.Copy).then_inc(setup_hi, 1)
            act.wait_ge(bias_done, 1)

            def high_part(name, i, used_by=None, bias_cols=None):
                if used_by and (not isinstance(i, int) or pj_use(used_by[0], used_by[1])):
                    act.wait_ge(pj_full[pj_bank(used_by[0])], pj_use(used_by[0], used_by[1]))
                act.wait_ge(pj_full[pj_bank(name)], pj_use(name, i))
                bank = pj[pj_bank(name)]
                hi = OP[name][0]
                if bias_cols is None:
                    last = nc.scalar.activation(hi[:, :, :].rearrange("p k t -> p (k t)"), bank[:, :], ACT.Copy)
                else:
                    for k in range(KC):
                        last = nc.scalar.activation(hi[:, k, :], bank[:, k * TOK:(k + 1) * TOK], ACT.Identity,
                                                    bias=bias[:, bias_cols + k:bias_cols + k + 1])
                last.then_inc(hi_done[name], 1)

            def queries(a, i):
                name = f"{a}.Q"
                act.wait_ge(pj_full[pj_bank(name)], pj_use(name, i))
                bank = pj[pj_bank(name)]
                for e in range(2):
                    for m in range(KC):
                        b = 0.0 if a == "C" else qbias[:, "AB".index(a), e, m:m + 1]
                        last = nc.scalar.activation(q2[a][:, m, :, e, :],
                                                    bank[:, m * TOK:(m + 1) * TOK].rearrange("p (b q) -> p b q", b=UB),
                                                    ACT.Identity, bias=b, scale=qscale[:, e:e + 1])
                last.then_inc(pj_free[pj_bank(name)], 1)

            def keys(a, i):
                name = f"{a}.K"
                act.wait_ge(pj_full[pj_bank(name)], pj_use(name, i))
                bank = pj[pj_bank(name)]
                for m in range(KC):
                    last = nc.scalar.activation(kT[a][:, m, :], bank[:, m * TOK:(m + 1) * TOK], ACT.Identity,
                                                bias=bias[:, BK[a] + m:BK[a] + m + 1])
                last.then_inc(pj_free[pj_bank(name)], 1)

            def exps(a, i):
                for r in range(R):
                    act.wait_ge(shifted[a], R * unit(a, i) + r + 1)
                    p2 = prob[a][:, r, :, :].rearrange("p n k -> p (n k)")
                    nc.scalar.activation(p2, p2, ACT.Exp).then_inc(exped[a], 1)

            def turned_back(a, i):
                for r in range(R):
                    act.wait_ge(turned[a], R * unit(a, i) + r + 1)
                    nc.scalar.activation(prob[a][:, r, :, :].rearrange("p n k -> p (n k)"), s_bank[r][:, :],
                                         ACT.Copy).then_inc(turned_in[a], 1)

            def gelus(m, i):
                name = f"M.H{m}"
                u = unit("M", i)
                act.wait_ge(pj_full[pj_bank(name)], pj_use(name, i))
                if m >= 2:
                    act.wait_ge(h_lo_done, GELU * u + m - 1)
                elif not isinstance(i, int) or u:
                    act.wait_ge(h_lo_done, GELU * (u - 1) + m + 3)
                bank = pj[pj_bank(name)]
                for k in range(2):
                    c = BH + 2 * m + k
                    last = nc.scalar.activation(g[:, m % 2, k, :], bank[:, k * TOK:(k + 1) * TOK],
                                                ACT.Gelu_apprx_tanh, bias=bias[:, c:c + 1])
                last.then_inc(pj_free[pj_bank(name)], 1)

            def body(i):
                if active("C", i):
                    high_part("C.xT", i, ("B.V", i - 1))
                    high_part("C.zT", i, ("A.V", i - 1))
                    queries("C", i)
                    keys("C", i)
                if active("B", i):
                    high_part("B.zT", i, ("B.Q", i - 1))
                    high_part("B.cT", i, ("C.Q", i))
                    queries("B", i)
                    keys("B", i)
                if active("M", i):
                    high_part("M.zT", i, ("M.H3", i - 1))
                if active("C", i):
                    exps("C", i)
                    turned_back("C", i)
                    high_part("C.OT", i, ("A.AO", i - 1), BV["C"])
                if active("M", i):
                    for m in range(GELU):
                        gelus(m, i)
                if active("B", i):
                    exps("B", i)
                    turned_back("B", i)
                if active("A", i):
                    high_part("A.zT", i, ("C.V", i))
                    queries("A", i)
                    keys("A", i)
                if active("B", i):
                    high_part("B.OT", i, ("C.AO", i), BV["B"])
                if active("A", i):
                    exps("A", i)
                    turned_back("A", i)
                    high_part("A.OT", i, ("B.AO", i), BV["A"])

            run(act, body, 1, LAST)

        @block.vector
        def _(dve):
            for a in "ABC":
                last = nc.vector.memset(vz[a][:, :, :, :, :], 0.0)
            last.then_inc(zeroed, 1)
            dve.wait_ge(zeroed, 1)
            for a in "ABC":
                for b2 in range(TILE):
                    last = nc.vector.memset(vz[a][b2 * S:(b2 + 1) * S, :, :, b2, 2 * HD:VW], 1.0)
            last.then_inc(half_set, 1)
            dve.wait_ge(const_in, CONST)
            nc.vector.tensor_scalar(qscale[:, :], parity[:, :], HD ** -0.5, None, ALU.mult).then_inc(masks_done, 1)
            nc.vector.tensor_scalar(maskA_off[:, :, :], maskA[:, :, :], 1.0, OFF, ALU.subtract,
                                    ALU.mult).then_inc(masks_done, 1)

            def low_part_of_weight(n):
                group, name, scaled, w, kc = pieces[n]
                dve.wait_ge(setup_hi, n + 1)
                nc.vector.tensor_tensor(w_lo[name][:, :, :], w, w_hi[name][:, :, :].bitcast(F32),
                                        ALU.subtract).then_inc(setup_lo, 1)

            n_pe = 0
            for n, (group, name, scaled, w, kc) in enumerate(pieces):
                dve.wait_ge(stage_in[group], 16 * len(GROUPS[group]))
                if scaled in ("A", "B", "M", "C"):
                    n_pe += 1
                    dve.wait_ge(setup_pe, n_pe)
                    for k in range(kc):
                        last = nc.vector.tensor_scalar(w[:, k, :], w[:, k, :], lnvec[:, LN[scaled], 0, k:k + 1],
                                                       None, ALU.mult)
                elif scaled == "gate":
                    dve.wait_ge(gate_done, 1)
                    last = nc.vector.tensor_scalar(w, w, gate_t[:, 0:1], None, ALU.mult)
                if scaled:
                    last.then_inc(setup_scaled, 1)
                if n:
                    low_part_of_weight(n - 1)
            low_part_of_weight(len(pieces) - 1)
            dve.wait_ge(setup_pe, n_pe)
            dve.wait_ge(setup_pool, 1)
            nc.vector.tensor_tensor(bias[:, 0:20], pj[0][:, 0:20], bias_in[:, 0:20], ALU.add).then_inc(masks_done, 1)
            nc.vector.tensor_copy(bias[:, 20:24], bias_in[:, 20:24]).then_inc(masks_done, 1)
            dve.wait_ge(masks_done, 4)
            for n, a in enumerate("AB"):
                for e in range(2):
                    last = nc.vector.tensor_scalar(qbias[:, n, e, :], bias[:, BQ[a]:BQ[a] + KC],
                                                   qscale[:, e:e + 1], None, ALU.mult)
            last.then_inc(bias_done, 1)

            def low_part(name, i, bias_cols=None):
                dve.wait_ge(hi_done[name], unit(name[0], i) + 1)
                bank = pj[pj_bank(name)]
                hi, lo = OP[name]
                hi = hi[:, :, :].bitcast(F32)
                if bias_cols is None:
                    last = nc.vector.tensor_tensor(lo[:, :, :].rearrange("p k t -> p (k t)"), bank[:, :],
                                                   hi.rearrange("p k t -> p (k t)"), ALU.subtract)
                else:
                    for k in range(KC):
                        last = nc.vector.scalar_tensor_tensor(
                            lo[:, k, :], bank[:, k * TOK:(k + 1) * TOK], bias[:, bias_cols + k:bias_cols + k + 1],
                            hi[:, k, :], ALU.add, ALU.subtract)
                last.then_inc(pj_free[pj_bank(name)], 1)

            def value_rows(a, i):
                name = f"{a}.V"
                dve.wait_ge(pj_full[pj_bank(name)], pj_use(name, i))
                v = pj[pj_bank(name)][:, :].rearrange("p (t e g f) -> p t g e f", t=T, e=2, g=R * C2)
                for t in range(T):
                    for b2 in range(TILE):
                        rows_ = slice(b2 * S, (b2 + 1) * S)
                        dst = vz[a][rows_, t, :, b2, 0:2 * HD].rearrange("p g (e f) -> p g e f", e=2)
                        last = nc.vector.tensor_copy(dst, v[rows_, t])
                last.then_inc(pj_free[pj_bank(name)], 1)

            def mask_scores(a, r, i):
                dve.wait_ge(scored[a], R * unit(a, i) + r + 1)
                dst = prob[a][:, r, :, :].rearrange("p (t c) k -> p t c k", t=T)
                src = s_bank[r][:, :].rearrange("p (t c k) -> p t c k", t=T, c=C2)
                m, f = {"A": (maskA, ALU.mult), "B": (maskB, ALU.mult), "C": (maskC_off, ALU.add)}[a]
                if a == "A":
                    m = m[:, :, :].rearrange("p (o b) k -> p o (b k)", o=1).unsqueeze(2).broadcast_to(
                        [P, T, C2, TILE * S])
                else:
                    m = m[:, :, :].rearrange("p (t b) k -> p t (b k)", t=T).unsqueeze(2).broadcast_to(
                        [P, T, C2, TILE * S])
                nc.vector.tensor_tensor(dst, src, m, f).then_inc(masked[a], 1)

            def row_max(a, r, i):
                dve.wait_ge((masked if a == "C" else offset)[a], R * unit(a, i) + r + 1)
                nc.vector.tensor_reduce(rmax[a][:, r, :], prob[a][:, r, :, :].rearrange("p n (b k) -> p (n b) k", b=TILE),
                                        AX.X, ALU.max).then_inc(maxed[a], 1)

            def normalise(a, i):
                u = unit(a, i)
                for r in range(R):
                    dve.wait_ge(summed[a], R * u + r + 1)
                    pv = pv_bank[r % 2][:, 0:UB * C2 * VW].rearrange("p (n v) -> p n v", v=VW)
                    nc.vector.reciprocal(rden[a][:, r, :], pv[:, :, 2 * HD]).then_inc(inverted[a], 1)
                    dve.wait_ge(inverted[a], R * u + r + 1)
                    for e in range(2):
                        last = nc.vector.tensor_tensor(
                            o[:, :, e, r, :].rearrange("p b (c f) -> p b c f", c=C2),
                            pv[:, :, e * HD:(e + 1) * HD].rearrange("p (b c) f -> p b c f", c=C2),
                            rden[a][:, r, :].rearrange("p (b c) -> p b c", c=C2).unsqueeze(3).broadcast_to(
                                [P, UB, C2, HD]), ALU.mult)
                    last.then_inc(normed[a], 1)

            def tokens_out(stage, bank_use, dst, residual, i):
                dve.wait_ge(pj_full[pj_bank(bank_use)], pj_use(bank_use, i))
                nc.vector.tensor_tensor(dst[:, :, :].rearrange("p t c -> p (t c)"), pj[pj_bank(bank_use)][:, :],
                                        residual[:, :, :].rearrange("p t c -> p (t c)"),
                                        ALU.add).then_inc(tokens[stage], 1)

            def layer_norm(l, src, u, src_wait=None):
                n = LN[l]
                for t in range(T):
                    last = nc.vector.bn_stats(stats[:, n, t, :], src[:, t, :])
                last.then_inc(ln_stats[l], 1)
                dve.wait_ge(setup_pool, 1)
                dve.wait_ge(ln_stats[l], u + 1)
                for t in range(T):
                    last = nc.vector.bn_aggr(mv[:, n, t, :], stats[:, n, t, :])
                last.then_inc(ln_mv[l], 1)
                dve.wait_ge(ln_rstd[l], u + 1)
                for t in range(T):
                    last = nc.vector.tensor_scalar(z[l][:, t, :], src[:, t, :], mv[:, n, t, 0:1],
                                                   rstd[:, n, t:t + 1], ALU.subtract, ALU.mult)
                last.then_inc(ln_done[l], 1)

            def body(i):
                if active("C", i):
                    low_part("C.xT", i)
                    low_part("C.zT", i)
                    value_rows("C", i)
                    dve.wait_ge(maskc_off_s, unit("C", i) + 1)
                    for r in range(R):
                        mask_scores("C", r, i)
                    for r in range(R):
                        row_max("C", r, i)
                if active("B", i):
                    low_part("B.zT", i)
                    low_part("B.cT", i)
                    value_rows("B", i)
                if active("M", i):
                    low_part("M.zT", i)
                if active("C", i):
                    normalise("C", i)
                if active("B", i):
                    u = unit("B", i)
                    dve.wait_ge(maskb_s, 32 * (u + 1))
                    if not isinstance(i, int) or u:
                        dve.wait_ge(offset["B"], R * u)
                    nc.vector.tensor_scalar(maskB_off[:, :, :], maskB[:, :, :], 1.0, OFF, ALU.subtract,
                                            ALU.mult).then_inc(maskb_off_s, 1)
                    for r in range(R):
                        mask_scores("B", r, i)
                    for r in range(R):
                        row_max("B", r, i)
                if active("C", i):
                    low_part("C.OT", i, BV["C"])
                if active("M", i):
                    high_h(0, i)
                    high_h(1, i)
                if active("C", i):
                    u = unit("C", i)
                    if not isinstance(i, int) or u:
                        dve.wait_ge(stored, 16 * u)
                    tokens_out("C", "C.AO", y, x3, i)
                    dve.wait_ge(tokens["C"], u + 1)
                    free("C.AO")
                if active("M", i):
                    high_h(2, i)
                    high_h(3, i)
                if active("B", i):
                    normalise("B", i)
                if active("A", i):
                    low_part("A.zT", i)
                    value_rows("A", i)
                    for r in range(R):
                        mask_scores("A", r, i)
                    for r in range(R):
                        row_max("A", r, i)
                if active("B", i):
                    low_part("B.OT", i, BV["B"])
                if active("M", i):
                    tokens_out("M", "M.Y", x3, xb["M"], i)
                    dve.wait_ge(tokens["M"], unit("M", i) + 1)
                    free("M.Y")
                if active("B", i):
                    u = unit("B", i)
                    if not isinstance(i, int) or unit("A", i):
                        dve.wait_ge(xb_done["B"], u + 1)
                    tokens_out("B", "B.AO", x12, xb["B"], i)
                    dve.wait_ge(tokens["B"], u + 1)
                    free("B.AO")
                    layer_norm("M", x12, u)
                if active("A", i):
                    u = unit("A", i)
                    normalise("A", i)
                    low_part("A.OT", i, BV["A"])
                    if not isinstance(i, int) or active("B", i):
                        dve.wait_ge(xb_done["M"], unit("B", i) + 1)
                    tokens_out("A", "A.AO", x12, xb["A"], i)
                    dve.wait_ge(tokens["A"], u + 1)
                    free("A.AO")
                    layer_norm("B", x12, u)
                if active("P", i):
                    u = unit("P", i)
                    dve.wait_ge(x_in_s, 16 * (u + 1))
                    layer_norm("A", x_in, u)
                if active("M", i):
                    u = unit("M", i)
                    dve.wait_ge(maskc_s, 16 * (u + 1))
                    nc.vector.tensor_scalar(maskC_off[:, :, :], maskC[:, :, :], 1.0, FAR, ALU.subtract,
                                            ALU.mult).then_inc(maskc_off_s, 1)
                    dve.wait_ge(ctxc_s, 16 * (u + 1))
                    layer_norm("C", ctx_c, u)

            def free(name):
                nc.vector.nop().then_inc(pj_free[pj_bank(name)], 1)

            def high_h(m, i):
                u = unit("M", i)
                if not isinstance(i, int) or u:
                    dve.wait_ge(pj_full[pj_bank("M.Y")], pj_use("M.Y", i - 1))
                dve.wait_ge(pj_free[pj_bank(f"M.H{m}")], pj_use(f"M.H{m}", i))
                nc.vector.tensor_copy(h_hi[:, 2 * m:2 * m + 2, :], g[:, m % 2, :, :]).then_inc(h_hi_done, 1)

            run(dve, body, 0, LAST)

        @block.gpsimd
        def _(pool):
            nc.gpsimd.memset(eps[:, :], EPS)
            nc.gpsimd.memset(half[:, :], -0.5).then_inc(half_set, 1)
            pool.wait_ge(const_in, CONST)
            nc.gpsimd.memset(bias_in[:, 16:20], 0.0).then_inc(setup_pool, 1)
            pool.wait_ge(half_set, 2)
            pool.wait_ge(masks_done, 2)

            def rstds(l, i, stage):
                n, u = LN[l], unit(stage, i)
                pool.wait_ge(ln_mv[l], u + 1)
                nc.gpsimd.tensor_tensor(veps[:, n, :], mv[:, n, :, 1], eps[:, :], ALU.add).then_inc(ln_eps[l], 1)
                pool.wait_ge(ln_eps[l], u + 1)
                nc.gpsimd.tensor_tensor(rstd[:, n, :], veps[:, n, :], half[:, :], ALU.pow).then_inc(ln_rstd[l], 1)

            def residual(stage, src, k, u):
                nc.gpsimd.tensor_tensor(xb[stage][:, :, :], src[:, :, :],
                                        brow[:, k, :].unsqueeze(1).broadcast_to([P, T, H]),
                                        ALU.add).then_inc(xb_done[stage], 1)

            def add_offset(a, i):
                u = unit(a, i)
                for r in range(R):
                    pool.wait_ge(masked[a], R * u + r + 1)
                    for t in range(T):
                        p3 = prob[a][:, r, t * C2:(t + 1) * C2, :]
                        m = maskA_off[:, :, :] if a == "A" else maskB_off[:, t * TILE:(t + 1) * TILE, :]
                        last = nc.gpsimd.tensor_tensor(
                            p3, p3, m.rearrange("p b k -> p (b k)").unsqueeze(1).broadcast_to([P, C2, TILE * S]),
                            ALU.add)
                    last.then_inc(offset[a], 1)

            def shift(a, i):
                u = unit(a, i)
                for r in range(R):
                    pool.wait_ge(maxed[a], R * u + r + 1)
                    p3 = prob[a][:, r, :, :].rearrange("p n (b k) -> p (n b) k", b=TILE)
                    nc.gpsimd.tensor_tensor(p3, p3, rmax[a][:, r, :].unsqueeze(2).broadcast_to(
                        [P, T * C2 * TILE, S]), ALU.subtract).then_inc(shifted[a], 1)

            def low_h(m, i):
                u = unit("M", i)
                pool.wait_ge(h_hi_done, GELU * u + m + 1)
                nc.gpsimd.tensor_tensor(h_lo[:, 2 * m:2 * m + 2, :], g[:, m % 2, :, :],
                                        h_hi[:, 2 * m:2 * m + 2, :].bitcast(F32), ALU.subtract).then_inc(h_lo_done, 1)

            def body(i):
                if active("C", i):
                    shift("C", i)
                if active("B", i):
                    pool.wait_ge(maskb_off_s, unit("B", i) + 1)
                    add_offset("B", i)
                    shift("B", i)
                if active("M", i):
                    for m in range(GELU):
                        low_h(m, i)
                if active("A", i):
                    add_offset("A", i)
                    shift("A", i)
                if active("B", i):
                    u = unit("B", i)
                    rstds("M", i, "B")
                    residual("M", x12, 2, u)
                if active("A", i):
                    u = unit("A", i)
                    rstds("B", i, "A")
                    residual("B", x12, 1, u)
                if active("P", i):
                    u = unit("P", i)
                    pool.wait_ge(x_in_s, 16 * (u + 1))
                    residual("A", x_in, 0, u)
                    rstds("A", i, "P")
                if active("M", i):
                    rstds("C", i, "M")

            run(pool, body, 0, LAST)


CONST = 16 * (2 + 3 + 3 + 1 + 2 * TILE)


def kernel(**inputs):
    import numpy as np
    import concourse.bacc as bacc
    from concourse.bass_utils import run_bass_kernel_spmd

    a = {k: np.asarray(v) for k, v in inputs.items()}
    L0, L1 = "L0_xattn_", "L1_xattn_"

    def by_parity(w):
        v = w.reshape(C2, R, 2, HD, *w.shape[1:])
        return v.transpose(2, 1, 0, 3, *range(4, v.ndim)).reshape(w.shape)

    def columns(vectors):
        return np.concatenate(vectors).reshape(-1, P).T

    feature = np.arange(P)
    arrays = {
        "x": a["x"], "ctx_2048": a["ctx_2048"], "mask_1x1xSxS2_fc1": a["mask_1x1xSxS2_fc1"],
        "mask_Bx1xSxS2_ff1": a["mask_Bx1xSxS2_ff1"], "mask_BxS2_bf1": a["mask_BxS2_bf1"],
        "identity": np.eye(P, dtype=np.float32),
        "parity": np.stack([feature // HD % 2 == e for e in range(2)], 1).astype(np.float32),
        "w_A_qkv": np.concatenate([a[L0 + "w_qkv"][:, :2 * H], by_parity(a[L0 + "w_qkv"][:, 2 * H:].T).T], 1),
        "w_A_o": by_parity(a[L0 + "w_ao"]),
        "w_B_q": a[L0 + "w_q"],
        "w_B_kv": np.concatenate([a[L0 + "w_kv"][:, :H], by_parity(a[L0 + "w_kv"][:, H:].T).T], 1),
        "w_B_o": by_parity(a[L0 + "w_co"]),
        "ln_vectors": columns([a[L0 + "ln1_s"], a[L0 + "ln1_b"], a[L0 + "ln2_s"], a[L0 + "ln2_b"],
                               a[L0 + "ln3_s"], a[L0 + "ln3_b"], a[L1 + "ln_gamma"], a[L1 + "ln_beta"]]),
        "biases": columns([a[L0 + "b_qkv"][:2 * H], by_parity(a[L0 + "b_qkv"][2 * H:]), a[L0 + "b_q"],
                           a[L0 + "b1"], a[L0 + "b_kv"][:H], by_parity(a[L0 + "b_kv"][H:])]),
        "w_M_1": a[L0 + "w1"], "w_M_2": a[L0 + "w2"],
        "w_C_q": a[L1 + "Wq"].T, "w_C_k": a[L1 + "Wk"].T, "w_C_v": by_parity(a[L1 + "Wv"]).T,
        "w_C_o": by_parity(a[L1 + "Wo"].T),
    }
    for n in ("b2", "b_ao", "b_co"):
        arrays[L0 + n] = a[L0 + n]
    arrays[L1 + "gate"] = a[L1 + "gate"]
    nc = bacc.Bacc("TRN2", target_bir_lowering=False, num_devices=1)
    arrays = {k: np.ascontiguousarray(v) for k, v in arrays.items()}
    d = {k: nc.dram_tensor("in_" + k, v.shape, mybir.dt.from_np(v.dtype), kind="ExternalInput").ap()
         for k, v in arrays.items()}
    out = nc.dram_tensor("out", (NB, S, H), F32, kind="ExternalOutput").ap()
    build(nc, d, out)
    r = run_bass_kernel_spmd(nc, [{"in_" + k: v for k, v in arrays.items()}], core_ids=[0])
    return r.results[0]["out"]
```

```python
from contextlib import ExitStack

import concourse.bass as bass
from concourse import mybir

F32 = mybir.dt.float32
F32R = mybir.dt.float32r
U8 = mybir.dt.uint8
ALU = mybir.AluOpType
ACT = mybir.ActivationFunctionType
AX = mybir.AxisListType

NB, S, H = 64, 64, 256
NH = 16
HD = H // NH
FF = 4 * H
P = 128
TILE = P // S
T = 2
UB = T * TILE
TOK = UB * S
U = NB // UB
KC = H // P
R = 4
BL = 4
NPAIR = NH // 2
HALVES = 2
VW = 2 * HD + 1
BANK = 512
EPS = 1e-5
OFF = 10000.0
FAR = 1e30

STAGES = "PABMC"
LAG = {s: n for n, s in enumerate(STAGES)}
FIRST = len(STAGES)
TAIL = len(STAGES) - 1
PJ = ["C.xT", "C.K", "B.cT", "C.Q", "M.zT", "A.zT", "B.V", "B.zT", "B.K", "B.Q", "M.H0", "M.H1",
      "M.H2", "A.K", "A.Q", "A.V", "M.H3", "C.OT", "M.cT", "C.AO", "M.Y0", "B.OT", "M.V", "B.AO",
      "A.OT", "M.Y1", "A.AO"]
PJ_BANKS = 4
S_USES = ["S_C", "S_B", "T_C", "S_A", "T_B", "T_A"]
ATT = "CBA"
GELU = 4


def unit(stage, i):
    return i - LAG[stage]


def active(stage, i):
    return not isinstance(i, int) or 0 <= unit(stage, i) < U


def pj_bank(name):
    return PJ.index(name) % PJ_BANKS


def pj_uses(b):
    return PJ[b::PJ_BANKS]


def pj_use(name, i):
    names = pj_uses(pj_bank(name))
    if isinstance(i, int):
        return sum(active(n[0], j) for j in range(i) for n in names) + sum(
            active(n[0], i) for n in names[:names.index(name) + 1])
    return pj_use(name, FIRST) + (i - FIRST) * len(names)


def score_use_before(use, i):
    k = S_USES.index(use)
    if not isinstance(i, int):
        n = S_USES[k - 1]
        return (n, unit(n[2], i) + 1) if k else (n, unit(n[2], i))
    done = [(n, unit(n[2], j) + 1) for j in range(i) for n in S_USES if active(n[2], j)]
    done += [(n, unit(n[2], i) + 1) for n in S_USES[:k] if active(n[2], i)]
    return done[-1] if done else None


def value_use(a, i):
    return ("M.V", i - 1) if a == "C" else (f"{a}.V", i)


def before(a, i):
    if not isinstance(i, int):
        n = ATT.index(a)
        return (ATT[n - 1], unit(ATT[n - 1], i) + 1) if n else (ATT[-1], unit(ATT[-1], i))
    done = [(x, unit(x, j) + 1) for j in range(i) for x in ATT if active(x, j)]
    done += [(x, unit(x, i) + 1) for x in ATT[:ATT.index(a)] if active(x, i)]
    return done[-1] if done else None


def build(nc, d, out):
    ctx = ExitStack()
    with ctx:
        def sb(name, shape, dt=F32):
            return ctx.enter_context(nc.sbuf_tensor(name, shape, dt))

        def ps(name):
            return ctx.enter_context(nc.psum_tensor(name, [P, BANK], F32))

        def sem(name):
            return ctx.enter_context(nc.semaphore(name))

        WCOLS = {"A_qkv": (3 * H, KC), "A_o": (H, KC), "B_q": (H, KC), "B_kv": (2 * H, KC),
                 "B_o": (H, KC), "M_1": (FF, KC), "M_2": (H, FF // P), "C_q": (H, KC),
                 "C_k": (H, KC), "C_v": (H, KC), "C_o": (H, KC)}
        w_hi = {n: sb(f"w_hi_{n}", [P, k, c], F32R) for n, (c, k) in WCOLS.items()}
        w_lo = {n: sb(f"w_lo_{n}", [P, k, c], F32R) for n, (c, k) in WCOLS.items()}

        ident = sb("ident", [P, P])
        parity = sb("parity", [P, 4])
        qscale = sb("qscale", [P, 2])
        lnvec = sb("lnvec", [P, 4, 2, KC])
        NBIAS, BC, BB = 24, 16, 20
        bias_in = sb("bias_in", [P, NBIAS])
        bias = sb("bias", [P, NBIAS])
        BQ, BK, BV, BH = {"A": 0, "B": 6}, {"A": 2, "B": 20, "C": 16}, {"A": 4, "B": 22, "C": 18}, 8
        qbias = sb("qbias", [P, 2, 2, KC])
        kbias = sb("kbias", [P, 3, 2, KC])
        brow = sb("brow", [P, 3, H])
        gate = sb("gate", [P, 1])
        gate_t = sb("gate_t", [P, 1])
        half = sb("half", [P, T])
        eps = sb("eps", [P, T])
        maskA = sb("maskA", [P, TILE, S])
        maskA_off = sb("maskA_off", [P, TILE, S])

        x_in = sb("x_in", [P, T, H])
        ctx_b = sb("ctx_b", [P, T, H])
        ctx_c = sb("ctx_c", [P, T, H])
        z = {"A": sb("z_A", [P, T, H]), "B": sb("z_B", [P, T, H]), "M": sb("z_M", [P, T, H]),
             "C": ctx_c}
        xb = {s: sb(f"xb_{s}", [P, T, H]) for s in "ABM"}
        x1 = sb("x1", [P, T, H])
        x2 = sb("x2", [P, T, H])
        x3 = sb("x3", [P, T, H])
        y = sb("y", [P, T, H])
        stats = sb("stats", [P, 4, T, 6])
        mv = sb("mv", [P, 4, T, 2])
        veps = sb("veps", [P, 4, T])
        rstd = sb("rstd", [P, 4, T])
        maskB = sb("maskB", [P, UB, S])
        maskB_off = sb("maskB_off", [P, UB, S])
        maskC = sb("maskC", [P, UB, S], U8)
        maskC_off = sb("maskC_off", [P, UB, S])
        op = {k: (sb(f"{k}_hi", [P, KC, TOK], F32R), sb(f"{k}_lo", [P, KC, TOK], F32R))
              for k in ("zT_A", "zT_B", "cT_C", "xT_C", "cT_B", "zT_M", "oT")}
        OP = {"A.zT": op["zT_A"], "M.cT": op["cT_C"], "B.zT": op["zT_B"],
              "B.cT": op["cT_B"], "C.xT": op["xT_C"], "M.zT": op["zT_M"],
              "A.OT": op["oT"], "B.OT": op["oT"], "C.OT": op["oT"]}
        q2 = sb("q2", [P, KC, UB, 2, S])
        k2 = sb("k2", [P, KC, UB, 2, S])
        vz = {a: sb(f"vz_{a}", [P, T, NPAIR, TILE, VW]) for a in "ABC"}
        prob = {"B": sb("prob_B", [P, R, BL, TILE * S]),
                "A": sb("prob_AC", [P, R, BL, TILE * S])}
        prob["C"] = prob["A"]
        rmax = {a: sb(f"rmax_{a}", [P, R, BL * TILE]) for a in "ABC"}
        rden = {a: sb(f"rden_{a}", [P, R, BL * TILE]) for a in "ABC"}
        o = sb("o", [P, UB, NPAIR, HD])
        g = sb("g", [P, GELU, 2, TOK])
        h_hi = sb("h_hi", [P, FF // P, TOK], F32R)
        h_lo = sb("h_lo", [P, FF // P, TOK], F32R)

        s_bank = [ps(f"s_bank{r}") for r in range(R)]
        pj = [ps(f"pj{n}") for n in range(PJ_BANKS)]

        const_in = sem("const_in")
        stage_in = [sem(f"stage_in{n}") for n in range(6)]
        setup_pe, setup_scaled, setup_hi, setup_lo = (sem(f"setup_{n}") for n in ("pe", "scaled", "hi", "lo"))
        bias_done, gate_done, masks_done = sem("bias_done"), sem("gate_done"), sem("masks_done")
        setup_pool = sem("setup_pool")
        half_set, zeroed = sem("half_set"), sem("zeroed")
        x_in_s, ctxb_s, ctxc_s, maskb_s, maskc_s = (sem(n) for n in ("x_in_s", "ctxb_s", "ctxc_s", "maskb_s", "maskc_s"))
        pj_full = [sem(f"pj_full{n}") for n in range(PJ_BANKS)]
        pj_free = [sem(f"pj_free{n}") for n in range(PJ_BANKS)]
        hi_done = {n: sem("hi_" + n.replace(".", "_")) for n in OP}
        scored = {a: sem(f"scored_{a}") for a in "ABC"}
        masked = {a: sem(f"masked_{a}") for a in "ABC"}
        offset = {a: sem(f"offset_{a}") for a in "AB"}
        maxed = {a: sem(f"maxed_{a}") for a in "ABC"}
        shifted = {a: sem(f"shifted_{a}") for a in "ABC"}
        exped = {a: sem(f"exped_{a}") for a in "ABC"}
        turned = {a: sem(f"turned_{a}") for a in "ABC"}
        turned_in = {a: sem(f"turned_in_{a}") for a in "ABC"}
        summed = {a: sem(f"summed_{a}") for a in "ABC"}
        inverted = {a: sem(f"inverted_{a}") for a in "ABC"}
        normed = {a: sem(f"normed_{a}") for a in "ABC"}
        gelued, h_hi_done, h_lo_done = sem("gelued"), sem("h_hi_done"), sem("h_lo_done")
        tokens = {s: sem(f"tokens_{s}") for s in "ABMC"}
        ln_stats = {s: sem(f"ln_stats_{s}") for s in "ABMC"}
        ln_mv = {s: sem(f"ln_mv_{s}") for s in "ABMC"}
        ln_eps = {s: sem(f"ln_eps_{s}") for s in "ABMC"}
        ln_rstd = {s: sem(f"ln_rstd_{s}") for s in "ABMC"}
        ln_done = {s: sem(f"ln_done_{s}") for s in "ABMC"}
        xb_done = {s: sem(f"xb_done_{s}") for s in "ABM"}
        maskb_off_s, maskc_off_s = sem("maskb_off_s"), sem("maskc_off_s")
        stored = sem("stored")

        LN = {"A": 0, "B": 1, "M": 2, "C": 3}

        x_d = d["x"].rearrange("(u t b) s c -> u (b s) t c", t=T, b=TILE)
        c_d = d["ctx_2048"].rearrange("(u t b) s c -> u (b s) t c", t=T, b=TILE)
        y_d = out.rearrange("(u t b) s c -> u (b s) t c", t=T, b=TILE)
        mB_d = d["mask_Bx1xSxS2_ff1"].rearrange("(u b) o q k -> u (o q) b k", b=UB)
        mC_d = d["mask_BxS2_bf1"].rearrange("(u o b) k -> u o (b k)", b=UB, o=1)

        def rows(name):
            return d[name].rearrange("(k p) c -> p k c", p=P)

        stage_buf = [prob["A"], prob["B"]]

        def staged(slot, at, k, c):
            flat = stage_buf[slot][:, :, :, :].rearrange("p a b c -> p (a b c)")
            return flat[:, at:at + k * c].rearrange("p (k c) -> p k c", k=k)

        GROUPS = [[("A_qkv", "A")],
                  [("A_o", None), ("B_q", "B"), ("B_o", None), ("C_q", None)],
                  [("B_kv", None), ("C_k", "C"), ("C_v", "C")],
                  [("M_1", "M")],
                  [("M_2", None)],
                  [("C_o", "gate")]]
        pieces = []
        for n, group in enumerate(GROUPS):
            at = 0
            for name, scaled in group:
                c, k = WCOLS[name]
                pieces.append((n, name, scaled, staged(n % 2, at, k, c), k))
                at += k * c
            assert at <= R * BL * TILE * S
        last_piece = [max(m for m, p in enumerate(pieces) if p[0] == n) for n in range(len(GROUPS))]
        N_CONST = 0

        def of_tile(m, a, r):
            t = r // HALVES
            m = m[:, :, :] if a == "A" else m[:, t * TILE:(t + 1) * TILE, :]
            return m.rearrange("p b k -> p (b k)").unsqueeze(1).broadcast_to([P, BL, TILE * S])

        block = ctx.enter_context(nc.Block())

        FEATURE = {"A.Q": ("A.zT", "A_qkv", 0), "A.K": ("A.zT", "A_qkv", H),
                   "B.Q": ("B.zT", "B_q", 0), "B.K": ("B.cT", "B_kv", 0),
                   "C.Q": ("C.xT", "C_q", 0), "C.K": ("M.cT", "C_k", 0),
                   **{f"M.H{m}": ("M.zT", "M_1", m * 2 * P) for m in range(GELU)}}
        TOKEN = {"A.V": ("A.zT", "A_qkv", 2 * H), "B.V": ("B.cT", "B_kv", H), "M.V": ("M.cT", "C_v", 0),
                 "A.AO": ("A.OT", "A_o", 0), "B.AO": ("B.OT", "B_o", 0), "C.AO": ("C.OT", "C_o", 0)}

        def run(eng, body, first, last):
            for i in range(first, min(FIRST, last + 1)):
                body(i)
            with eng.Fori(FIRST, U) as i:
                body(i)
            for i in range(U, last + 1):
                body(i)

        LAST = U - 1 + TAIL

        @block.sync
        def _(sp):
            n = [0]

            def const(dst, src):
                sp.dma_start(dst, src).then_inc(const_in, 16)
                n[0] += 16

            def load_group(k):
                for m, name, scaled, dst, kc in pieces:
                    if m == k:
                        sp.dma_start(dst, rows("w_" + name)).then_inc(stage_in[k], 16)

            def value(x):
                return x if isinstance(x, int) else sp.snap(x)

            def tokens_in(i):
                if active("P", i):
                    u = unit("P", i)
                    if not isinstance(i, int) or u:
                        sp.wait_ge(ln_done["A"], u)
                        sp.wait_ge(xb_done["A"], u)
                    sp.dma_start(x_in[:, :, :], x_d[i]).then_inc(x_in_s, 16)

            load_group(0)
            const(ident[:, :], d["identity"])
            const(parity[:, :], d["parity"])
            const(lnvec[:, :, :, :].rearrange("p n v k -> p (n v k)"), d["ln_vectors"])
            const(bias_in[:, 0:BC], d["biases"][:, 0:BC])
            const(bias_in[:, BB:NBIAS], d["biases"][:, BC:])
            for k, v in enumerate(("L0_xattn_b_ao", "L0_xattn_b_co", "L0_xattn_b2")):
                const(brow[:, k, :], d[v].rearrange("(o c) -> o c", o=1).broadcast_to([P, H]))
            const(gate[:, :], d["L1_xattn_gate"].rearrange("(o c) -> o c", o=1).broadcast_to([P, 1]))
            for half_p in range(2):
                for b in range(TILE):
                    const(maskA[half_p * S:(half_p + 1) * S, b, :], d["mask_1x1xSxS2_fc1"][0, 0])
            assert n[0] == CONST
            load_group(1)
            for k in range(2, len(GROUPS)):
                sp.wait_ge(setup_lo, last_piece[k - 2] + 1)
                load_group(k)

            def body(i):
                later = not isinstance(i, int)
                b_masked = value(R * unit("B", i))
                u_b, u_m, c_out = value(unit("B", i)), value(unit("M", i)), value(unit("C", i) + 1)
                if active("B", i):
                    u = u_b
                    if later or u:
                        sp.wait_ge(hi_done["B.cT"], u)
                    sp.dma_start(ctx_b[:, :, :], c_d[u]).then_inc(ctxb_s, 16)
                    if later or u:
                        sp.wait_ge(masked["B"], b_masked)
                        sp.wait_ge(maskb_off_s, u)
                    for hp in range(2):
                        sp.dma_start(maskB[hp * S:(hp + 1) * S, :, :], mB_d[u]).then_inc(maskb_s, 16)
                if active("M", i):
                    u = u_m
                    if later or u:
                        sp.wait_ge(maskc_off_s, u)
                        sp.wait_ge(hi_done["M.cT"], u)
                    sp.dma_start(ctx_c[:, :, :], c_d[u]).then_inc(ctxc_s, 16)
                    sp.dma_start(maskC[:, :, :].rearrange("p b k -> p (b k)"),
                                 mC_d[u].broadcast_to([P, UB * S])).then_inc(maskc_s, 16)
                tokens_in(i)
                if active("C", i):
                    sp.wait_ge(tokens["C"], c_out)
                    sp.dma_start(y_d[unit("C", i)], y[:, :, :]).then_inc(stored, 16)

            run(sp, body, 0, LAST)
            sp.wait_ge(stored, 16 * U)

        @block.tensor
        def _(pe):
            pe.wait_ge(const_in, CONST)
            pe.wait_ge(setup_pool, 1)
            first = True
            for n, (group, name, scaled, w, kc) in enumerate(pieces):
                if scaled not in ("A", "B", "M", "C"):
                    continue
                pe.wait_ge(stage_in[group], 16 * len(GROUPS[group]))
                shift = lnvec[:, LN[scaled], 1, :]
                cols = WCOLS[name][0]
                at = {"A_qkv": 0, "B_q": 6, "M_1": 8, "C_k": 16, "C_v": 18}[name]
                for m in range(cols // P):
                    is_v = name == "C_v" or (name == "A_qkv" and m >= 4)
                    for k in range(KC):
                        if is_v:
                            lhs = w[:, k, cols - H + m % 2 * P:cols - H + (m % 2 + 1) * P]
                        else:
                            lhs = w[:, k, m * P:(m + 1) * P]
                        last = nc.tensor.matmul(pj[0][:, at + m:at + m + 1], lhs, shift[:, k:k + 1],
                                                start=(k == 0), stop=(k == KC - 1))
                last.then_inc(setup_pe, 1)

            pe.wait_ge(setup_lo, len(pieces))
            pe.wait_ge(bias_done, 1)

            def claim(name, i):
                n = pj_use(name, i) - 1
                if not isinstance(n, int) or n:
                    pe.wait_ge(pj_free[pj_bank(name)], n)
                return pj[pj_bank(name)]

            def turn(name, src, i):
                bank = claim(name, i)
                for k in range(KC):
                    for t in range(T):
                        at = k * TOK + t * P
                        last = nc.tensor.transpose(bank[:, at:at + P], src[:, t, k * P:(k + 1) * P], ident[:, :])
                last.then_inc(pj_full[pj_bank(name)], 1)

            def parts(x, w):
                return ((x[0], w_hi[w]), (x[1], w_hi[w]), (x[0], w_lo[w]))

            def feature_major(name, i):
                src, w, col = FEATURE[name]
                j = i - 1 if (name, src) == ("C.K", "M.cT") else i
                pe.wait_ge(pj_free[pj_bank(src)], pj_use(src, j))
                bank = claim(name, i)
                for m in range(2):
                    n = 0
                    for k in range(KC):
                        for x, wt in parts(OP[src], w):
                            last = nc.tensor.matmul(bank[:, m * TOK:(m + 1) * TOK],
                                                    wt[:, k, col + m * P:col + (m + 1) * P], x[:, k, :],
                                                    start=(n == 0), stop=(n == 3 * KC - 1))
                            n += 1
                last.then_inc(pj_full[pj_bank(name)], 1)

            def token_major(name, i):
                src, w, col = TOKEN[name]
                pe.wait_ge(pj_free[pj_bank(src)], pj_use(src, i))
                bank = claim(name, i)
                for t in range(T):
                    n = 0
                    for k in range(KC):
                        for x, wt in parts(OP[src], w):
                            last = nc.tensor.matmul(bank[:, t * H:(t + 1) * H], x[:, k, t * P:(t + 1) * P],
                                                    wt[:, k, col:col + H],
                                                    start=(n == 0), stop=(n == 3 * KC - 1))
                            n += 1
                last.then_inc(pj_full[pj_bank(name)], 1)

            def mlp_out(t, i):
                u = unit("M", i)
                pe.wait_ge(h_lo_done, GELU * (u + 1))
                bank = claim(f"M.Y{t}", i)
                n = 0
                for k in range(FF // P):
                    for x, wt in ((h_hi, w_hi["M_2"]), (h_lo, w_hi["M_2"]), (h_hi, w_lo["M_2"])):
                        last = nc.tensor.matmul(bank[:, 0:H], x[:, k, t * P:(t + 1) * P],
                                                wt[:, k, :], start=(n == 0), stop=(n == 3 * (FF // P) - 1))
                        n += 1
                last.then_inc(pj_full[pj_bank(f"M.Y{t}")], 1)

            def wait_score_banks(use, i, r):
                if b := score_use_before(use, i):
                    read = masked if b[0][0] == "S" else normed
                    pe.wait_ge(read[b[0][2]], R * (b[1] - 1) + r + 1)

            def scores(a, i):
                for name in (f"{a}.Q", f"{a}.K"):
                    pe.wait_ge(pj_free[pj_bank(name)], pj_use(name, i))
                for t in range(T):
                    wait_score_banks(f"S_{a}", i, HALVES * (t + 1) - 1)
                    for c in range(KC):
                        for b2 in range(TILE):
                            for half in range(HALVES):
                                rows_ = slice(half * S, (half + 1) * S)
                                bank = s_bank[t * HALVES + half][:, :].rearrange(
                                    "p (c s b k) -> p c s b k", c=KC, s=2, b=TILE)
                                mm = nc.tensor.matmul(bank[:, c, :, b2, :],
                                                      q2[rows_, c, t * TILE + b2].rearrange("p e q -> p (e q)"),
                                                      k2[rows_, c, t * TILE + b2], start=True, stop=True)
                                if (c, b2) == (KC - 1, TILE - 1):
                                    mm.then_inc(scored[a], 1)

            def turn_probs(a, r, i):
                wait_score_banks(f"T_{a}", i, r)
                pe.wait_ge(exped[a], R * unit(a, i) + r + 1)
                for n in range(BL):
                    last = nc.tensor.transpose(s_bank[r][:, n * P:(n + 1) * P], prob[a][:, r, n, :], ident[:, :])
                last.then_inc(turned[a], 1)

            def values(a, r, i):
                u = unit(a, i)
                if r == 0:
                    name, j = value_use(a, i)
                    pe.wait_ge(pj_free[pj_bank(name)], pj_use(name, j))
                pe.wait_ge(turned_in[a], R * u + r + 1)
                t, half = divmod(r, HALVES)
                for n in range(BL):
                    last = nc.tensor.matmul(s_bank[r][:, n * TILE * VW:(n + 1) * TILE * VW],
                                            prob[a][:, r, n, :], vz[a][:, t, half * BL + n, :, :],
                                            start=True, stop=True)
                last.then_inc(summed[a], 1)

            def attend(a, i):
                for r in range(R):
                    turn_probs(a, r, i)
                for r in range(R):
                    values(a, r, i)

            def turn_out(a, i):
                name = f"{a}.OT"
                pe.wait_ge(normed[a], R * (unit(a, i) + 1))
                bank = claim(name, i)
                for b in range(UB):
                    last = nc.tensor.transpose(bank[:, b * P:(b + 1) * P],
                                               o[:, b].rearrange("p m f -> p (m f)"), ident[:, :])
                last.then_inc(pj_full[pj_bank(name)], 1)

            def body(i):
                if active("C", i):
                    pe.wait_ge(tokens["M"], T * (unit("C", i) + 1))
                    turn("C.xT", x3, i)
                    feature_major("C.K", i)
                if active("B", i):
                    pe.wait_ge(ctxb_s, 16 * (unit("B", i) + 1))
                    turn("B.cT", ctx_b, i)
                if active("C", i):
                    feature_major("C.Q", i)
                if active("M", i):
                    pe.wait_ge(ln_done["M"], unit("M", i) + 1)
                    turn("M.zT", z["M"], i)
                if active("A", i):
                    pe.wait_ge(ln_done["A"], unit("A", i) + 1)
                    turn("A.zT", z["A"], i)
                if active("B", i):
                    token_major("B.V", i)
                    pe.wait_ge(ln_done["B"], unit("B", i) + 1)
                    turn("B.zT", z["B"], i)
                if active("C", i):
                    scores("C", i)
                if active("B", i):
                    feature_major("B.K", i)
                    feature_major("B.Q", i)
                if active("M", i):
                    feature_major("M.H0", i)
                    feature_major("M.H1", i)
                if active("B", i):
                    scores("B", i)
                if active("M", i):
                    feature_major("M.H2", i)
                if active("C", i):
                    attend("C", i)
                if active("A", i):
                    feature_major("A.K", i)
                    feature_major("A.Q", i)
                    token_major("A.V", i)
                if active("M", i):
                    feature_major("M.H3", i)
                if active("C", i):
                    turn_out("C", i)
                if active("M", i):
                    pe.wait_ge(ln_done["C"], unit("M", i) + 1)
                    turn("M.cT", ctx_c, i)
                if active("A", i):
                    scores("A", i)
                if active("C", i):
                    token_major("C.AO", i)
                if active("B", i):
                    attend("B", i)
                if active("M", i):
                    mlp_out(0, i)
                if active("B", i):
                    turn_out("B", i)
                if active("M", i):
                    token_major("M.V", i)
                if active("A", i):
                    attend("A", i)
                if active("B", i):
                    token_major("B.AO", i)
                if active("A", i):
                    turn_out("A", i)
                if active("M", i):
                    mlp_out(1, i)
                if active("A", i):
                    token_major("A.AO", i)

            run(pe, body, 1, LAST)

        @block.scalar
        def _(act):
            act.wait_ge(const_in, CONST)
            nc.scalar.activation(gate_t[:, :], gate[:, :], ACT.Tanh).then_inc(gate_done, 1)
            for n, (group, name, scaled, w, kc) in enumerate(pieces):
                act.wait_ge(stage_in[group], 16 * len(GROUPS[group]))
                if scaled:
                    act.wait_ge(setup_scaled, sum(bool(p[2]) for p in pieces[:n + 1]))
                nc.scalar.activation(w_hi[name][:, :, :], w, ACT.Copy).then_inc(setup_hi, 1)
            act.wait_ge(bias_done, 1)

            def high_part(name, i, used_by=None, bias_cols=None):
                if used_by and (not isinstance(i, int) or pj_use(used_by[0], used_by[1])):
                    act.wait_ge(pj_full[pj_bank(used_by[0])], pj_use(used_by[0], used_by[1]))
                act.wait_ge(pj_full[pj_bank(name)], pj_use(name, i))
                bank = pj[pj_bank(name)]
                hi = OP[name][0]
                if bias_cols is None:
                    last = nc.scalar.activation(hi[:, :, :].rearrange("p k t -> p (k t)"), bank[:, :], ACT.Copy)
                else:
                    turned_o = bank[:, :].rearrange("p (b e q) -> p e b q", b=UB, e=2)
                    for e in range(KC):
                        last = nc.scalar.activation(hi[:, e, :].rearrange("p (b q) -> p b q", b=UB), turned_o[:, e],
                                                    ACT.Identity, bias=bias[:, bias_cols + e:bias_cols + e + 1])
                last.then_inc(hi_done[name], 1)

            def wait_scores_before(a, i):
                if b := before(a, i):
                    act.wait_ge(scored[b[0]], R * b[1])

            def queries(a, i):
                name = f"{a}.Q"
                act.wait_ge(pj_full[pj_bank(name)], pj_use(name, i))
                q_all = pj[pj_bank(name)][:, :].rearrange("p (m b q) -> p m b q", m=KC, b=UB)
                for e in range(2):
                    if a == "C":
                        last = nc.scalar.activation(q2[:, :, :, e, :], q_all, ACT.Copy, scale=qscale[:, e:e + 1])
                    else:
                        for m in range(KC):
                            last = nc.scalar.activation(q2[:, m, :, e, :], q_all[:, m], ACT.Identity,
                                                        bias=qbias[:, "AB".index(a), e, m:m + 1],
                                                        scale=qscale[:, e:e + 1])
                last.then_inc(pj_free[pj_bank(name)], 1)

            def keys(a, i):
                name = f"{a}.K"
                wait_scores_before(a, i)
                act.wait_ge(pj_full[pj_bank(name)], pj_use(name, i))
                k_all = pj[pj_bank(name)][:, :].rearrange("p (m b k) -> p m b k", m=KC, b=UB)
                for s in range(2):
                    for m in range(KC):
                        last = nc.scalar.activation(k2[:, m, :, s, :], k_all[:, m], ACT.Identity,
                                                    bias=kbias[:, "ABC".index(a), s, m:m + 1],
                                                    scale=parity[:, 2 + s:3 + s])
                last.then_inc(pj_free[pj_bank(name)], 1)

            def exps(a, i):
                for r in range(R):
                    act.wait_ge(shifted[a], R * unit(a, i) + r + 1)
                    p2 = prob[a][:, r, :, :].rearrange("p n k -> p (n k)")
                    nc.scalar.activation(p2, p2, ACT.Exp).then_inc(exped[a], 1)

            def turned_back(a, i):
                for r in range(R):
                    act.wait_ge(turned[a], R * unit(a, i) + r + 1)
                    nc.scalar.activation(prob[a][:, r, :, :].rearrange("p n k -> p (n k)"), s_bank[r][:, :],
                                         ACT.Copy).then_inc(turned_in[a], 1)

            def gelus(m, i):
                name = f"M.H{m}"
                u = unit("M", i)
                act.wait_ge(pj_full[pj_bank(name)], pj_use(name, i))
                if not isinstance(i, int) or u:
                    act.wait_ge(h_lo_done, GELU * (u - 1) + m + 1)
                bank = pj[pj_bank(name)]
                for k in range(2):
                    c = BH + 2 * m + k
                    last = nc.scalar.activation(g[:, m, k, :], bank[:, k * TOK:(k + 1) * TOK],
                                                ACT.Gelu_apprx_tanh, bias=bias[:, c:c + 1])
                last.then_inc(pj_free[pj_bank(name)], 1)

            def body(i):
                if active("C", i):
                    high_part("C.xT", i, ("C.Q", i - 1))
                    keys("C", i)
                if active("B", i):
                    high_part("B.cT", i, ("B.K", i - 1))
                if active("C", i):
                    queries("C", i)
                if active("M", i):
                    high_part("M.zT", i, ("M.H3", i - 1))
                if active("A", i):
                    high_part("A.zT", i, ("A.V", i - 1))
                if active("B", i):
                    high_part("B.zT", i, ("B.Q", i - 1))
                    keys("B", i)
                    queries("B", i)
                if active("C", i):
                    exps("C", i)
                if active("M", i):
                    for m in range(GELU - 1):
                        gelus(m, i)
                if active("C", i):
                    turned_back("C", i)
                if active("A", i):
                    keys("A", i)
                    queries("A", i)
                if active("M", i):
                    gelus(GELU - 1, i)
                if active("C", i):
                    high_part("C.OT", i, ("A.AO", i - 1), BV["C"])
                if active("M", i):
                    high_part("M.cT", i, ("C.K", i))
                if active("B", i):
                    exps("B", i)
                    turned_back("B", i)
                if active("A", i):
                    exps("A", i)
                if active("B", i):
                    high_part("B.OT", i, ("C.AO", i), BV["B"])
                if active("A", i):
                    turned_back("A", i)
                    high_part("A.OT", i, ("B.AO", i), BV["A"])

            run(act, body, 1, LAST)

        @block.vector
        def _(dve):
            for a in "ABC":
                last = nc.vector.memset(vz[a][:, :, :, :, :], 0.0)
            last.then_inc(zeroed, 1)
            dve.wait_ge(zeroed, 1)
            for a in "ABC":
                for b2 in range(TILE):
                    last = nc.vector.memset(vz[a][b2 * S:(b2 + 1) * S, :, :, b2, 2 * HD:VW], 1.0)
            last.then_inc(half_set, 1)
            dve.wait_ge(const_in, CONST)
            nc.vector.tensor_scalar(qscale[:, :], parity[:, 0:2], HD ** -0.5, None, ALU.mult).then_inc(masks_done, 1)
            nc.vector.tensor_scalar(maskA_off[:, :, :], maskA[:, :, :], 1.0, OFF, ALU.subtract,
                                    ALU.mult).then_inc(masks_done, 1)

            def low_part_of_weight(n):
                group, name, scaled, w, kc = pieces[n]
                dve.wait_ge(setup_hi, n + 1)
                nc.vector.tensor_tensor(w_lo[name][:, :, :], w, w_hi[name][:, :, :].bitcast(F32),
                                        ALU.subtract).then_inc(setup_lo, 1)

            n_pe = 0
            for n, (group, name, scaled, w, kc) in enumerate(pieces):
                dve.wait_ge(stage_in[group], 16 * len(GROUPS[group]))
                if scaled in ("A", "B", "M", "C"):
                    n_pe += 1
                    dve.wait_ge(setup_pe, n_pe)
                    for k in range(kc):
                        last = nc.vector.tensor_scalar(w[:, k, :], w[:, k, :], lnvec[:, LN[scaled], 0, k:k + 1],
                                                       None, ALU.mult)
                elif scaled == "gate":
                    dve.wait_ge(gate_done, 1)
                    last = nc.vector.tensor_scalar(w, w, gate_t[:, 0:1], None, ALU.mult)
                if scaled:
                    last.then_inc(setup_scaled, 1)
                if n:
                    low_part_of_weight(n - 1)
            low_part_of_weight(len(pieces) - 1)
            dve.wait_ge(setup_pe, n_pe)
            dve.wait_ge(setup_pool, 1)
            nc.vector.tensor_tensor(bias[:, 0:20], pj[0][:, 0:20], bias_in[:, 0:20], ALU.add).then_inc(masks_done, 1)
            nc.vector.tensor_copy(bias[:, 20:24], bias_in[:, 20:24]).then_inc(masks_done, 1)
            dve.wait_ge(masks_done, 4)
            for n, a in enumerate("AB"):
                for e in range(2):
                    last = nc.vector.tensor_scalar(qbias[:, n, e, :], bias[:, BQ[a]:BQ[a] + KC],
                                                   qscale[:, e:e + 1], None, ALU.mult)
            for n, a in enumerate("ABC"):
                for s in range(2):
                    last = nc.vector.tensor_scalar(kbias[:, n, s, :], bias[:, BK[a]:BK[a] + KC],
                                                   parity[:, 2 + s:3 + s], None, ALU.mult)
            last.then_inc(bias_done, 1)

            def low_part(name, i, bias_cols=None):
                dve.wait_ge(hi_done[name], unit(name[0], i) + 1)
                bank = pj[pj_bank(name)]
                hi, lo = OP[name]
                hi = hi[:, :, :].bitcast(F32)
                if bias_cols is None:
                    last = nc.vector.tensor_tensor(lo[:, :, :].rearrange("p k t -> p (k t)"), bank[:, :],
                                                   hi.rearrange("p k t -> p (k t)"), ALU.subtract)
                else:
                    turned_o = bank[:, :].rearrange("p (b e q) -> p e b q", b=UB, e=2)
                    for e in range(KC):
                        last = nc.vector.scalar_tensor_tensor(
                            lo[:, e, :].rearrange("p (b q) -> p b q", b=UB), turned_o[:, e],
                            bias[:, bias_cols + e:bias_cols + e + 1],
                            hi[:, e, :].rearrange("p (b q) -> p b q", b=UB), ALU.add, ALU.subtract)
                last.then_inc(pj_free[pj_bank(name)], 1)

            def value_rows(a, name, i):
                dve.wait_ge(pj_full[pj_bank(name)], pj_use(name, i))
                v = pj[pj_bank(name)][:, :].rearrange("p (t e m f) -> p t m e f", t=T, e=2, m=NPAIR)
                for t in range(T):
                    for b2 in range(TILE):
                        rows_ = slice(b2 * S, (b2 + 1) * S)
                        dst = vz[a][rows_, t, :, b2, 0:2 * HD].rearrange("p m (e f) -> p m e f", e=2)
                        last = nc.vector.tensor_copy(dst, v[rows_, t])
                last.then_inc(pj_free[pj_bank(name)], 1)

            def mask_scores(a, r, i):
                dve.wait_ge(scored[a], R * unit(a, i) + r + 1)
                m, f = {"A": (maskA, ALU.mult), "B": (maskB, ALU.mult), "C": (maskC_off, ALU.add)}[a]
                nc.vector.tensor_tensor(prob[a][:, r, :, :], s_bank[r][:, :].rearrange("p (n k) -> p n k", n=BL),
                                        of_tile(m, a, r), f).then_inc(masked[a], 1)

            def row_max(a, r, i):
                dve.wait_ge((masked if a == "C" else offset)[a], R * unit(a, i) + r + 1)
                nc.vector.tensor_reduce(rmax[a][:, r, :], prob[a][:, r, :, :].rearrange("p n (b k) -> p (n b) k", b=TILE),
                                        AX.X, ALU.max).then_inc(maxed[a], 1)

            def normalise(a, i, rs=range(R)):
                u = unit(a, i)
                for r in rs:
                    dve.wait_ge(summed[a], R * u + r + 1)
                    t, half = divmod(r, HALVES)
                    sums = s_bank[r][:, 0:BL * TILE * VW].rearrange("p (n v) -> p n v", v=VW)
                    nc.vector.reciprocal(rden[a][:, r, :], sums[:, :, 2 * HD]).then_inc(inverted[a], 1)
                    dve.wait_ge(inverted[a], R * u + r + 1)
                    for e in range(2):
                        rows_ = slice(e * S, (e + 1) * S)
                        last = nc.vector.tensor_tensor(
                            o[rows_, t * TILE:(t + 1) * TILE, half * BL:(half + 1) * BL, :],
                            sums[rows_, :, e * HD:(e + 1) * HD].rearrange("p (n b) f -> p b n f", b=TILE),
                            rden[a][rows_, r, :].rearrange("p (n b) -> p b n", b=TILE).unsqueeze(3).broadcast_to(
                                [S, TILE, BL, HD]), ALU.mult)
                    last.then_inc(normed[a], 1)

            def tokens_out(stage, bank_use, dst, residual, i):
                dve.wait_ge(pj_full[pj_bank(bank_use)], pj_use(bank_use, i))
                nc.vector.tensor_tensor(dst[:, :, :].rearrange("p t c -> p (t c)"), pj[pj_bank(bank_use)][:, :],
                                        residual[:, :, :].rearrange("p t c -> p (t c)"),
                                        ALU.add).then_inc(tokens[stage], 1)

            def mlp_tokens(t, i):
                name = f"M.Y{t}"
                dve.wait_ge(pj_full[pj_bank(name)], pj_use(name, i))
                nc.vector.tensor_tensor(x3[:, t, :], pj[pj_bank(name)][:, 0:H], xb["M"][:, t, :],
                                        ALU.add).then_inc(tokens["M"], 1)
                dve.wait_ge(tokens["M"], T * unit("M", i) + t + 1)
                free(name)

            def moments(l, src, u):
                n = LN[l]
                for t in range(T):
                    last = nc.vector.bn_stats(stats[:, n, t, :], src[:, t, :])
                last.then_inc(ln_stats[l], 1)
                dve.wait_ge(setup_pool, 1)
                dve.wait_ge(ln_stats[l], u + 1)
                for t in range(T):
                    last = nc.vector.bn_aggr(mv[:, n, t, :], stats[:, n, t, :])
                last.then_inc(ln_mv[l], 1)

            def normalised(l, src, u):
                n = LN[l]
                dve.wait_ge(ln_rstd[l], u + 1)
                for t in range(T):
                    last = nc.vector.tensor_scalar(z[l][:, t, :], src[:, t, :], mv[:, n, t, 0:1],
                                                   rstd[:, n, t:t + 1], ALU.subtract, ALU.mult)
                last.then_inc(ln_done[l], 1)

            def body(i):
                if active("C", i):
                    low_part("C.xT", i)
                if active("B", i):
                    dve.wait_ge(tokens["A"], unit("B", i) + 1)
                    moments("B", x1, unit("B", i))
                    low_part("B.cT", i)
                    normalised("B", x1, unit("B", i))
                if active("M", i):
                    low_part("M.zT", i)
                if active("A", i):
                    low_part("A.zT", i)
                if active("B", i):
                    low_part("B.zT", i)
                if active("C", i):
                    dve.wait_ge(maskc_off_s, unit("C", i) + 1)
                    for r in range(R):
                        mask_scores("C", r, i)
                if active("B", i):
                    value_rows("B", "B.V", i)
                if active("C", i):
                    for r in range(R):
                        row_max("C", r, i)
                if active("M", i):
                    u = unit("M", i)
                    dve.wait_ge(maskc_s, 16 * (u + 1))
                    nc.vector.tensor_scalar(maskC_off[:, :, :], maskC[:, :, :], 1.0, FAR, ALU.subtract,
                                            ALU.mult).then_inc(maskc_off_s, 1)
                    dve.wait_ge(ctxc_s, 16 * (u + 1))
                    moments("C", ctx_c, u)
                if active("B", i):
                    u = unit("B", i)
                    dve.wait_ge(maskb_s, 32 * (u + 1))
                    if not isinstance(i, int) or u:
                        dve.wait_ge(offset["B"], R * u)
                    nc.vector.tensor_scalar(maskB_off[:, :, :], maskB[:, :, :], 1.0, OFF, ALU.subtract,
                                            ALU.mult).then_inc(maskb_off_s, 1)
                    for r in range(R):
                        mask_scores("B", r, i)
                if active("P", i):
                    dve.wait_ge(x_in_s, 16 * (unit("P", i) + 1))
                    moments("A", x_in, unit("P", i))
                for n in range(R):
                    if active("B", i):
                        row_max("B", n, i)
                    if active("M", i) and n < GELU - 1:
                        high_h(n, i)
                if active("M", i):
                    normalised("C", ctx_c, unit("M", i))
                if active("C", i):
                    normalise("C", i)
                if active("P", i):
                    normalised("A", x_in, unit("P", i))
                if active("A", i):
                    value_rows("A", "A.V", i)
                if active("M", i):
                    high_h(GELU - 1, i)
                if active("C", i):
                    low_part("C.OT", i, BV["C"])
                if active("M", i):
                    low_part("M.cT", i)
                if active("A", i):
                    for r in range(R):
                        mask_scores("A", r, i)
                if active("C", i):
                    u = unit("C", i)
                    if not isinstance(i, int) or u:
                        dve.wait_ge(stored, 16 * u)
                    tokens_out("C", "C.AO", y, x3, i)
                    dve.wait_ge(tokens["C"], u + 1)
                    free("C.AO")
                for r in range(R):
                    if active("A", i):
                        row_max("A", r, i)
                    if active("B", i):
                        normalise("B", i, [r])
                if active("M", i):
                    dve.wait_ge(xb_done["M"], unit("M", i) + 1)
                    mlp_tokens(0, i)
                if active("B", i):
                    low_part("B.OT", i, BV["B"])
                if active("M", i):
                    value_rows("C", "M.V", i)
                if active("A", i):
                    normalise("A", i)
                if active("B", i):
                    u = unit("B", i)
                    dve.wait_ge(xb_done["B"], u + 1)
                    if not isinstance(i, int) or u:
                        dve.wait_ge(xb_done["M"], u)
                    tokens_out("B", "B.AO", x2, xb["B"], i)
                    dve.wait_ge(tokens["B"], u + 1)
                    free("B.AO")
                    moments("M", x2, u)
                if active("A", i):
                    low_part("A.OT", i, BV["A"])
                if active("B", i):
                    normalised("M", x2, unit("B", i))
                if active("M", i):
                    mlp_tokens(1, i)
                if active("A", i):
                    u = unit("A", i)
                    dve.wait_ge(xb_done["A"], u + 1)
                    if not isinstance(i, int) or u:
                        dve.wait_ge(xb_done["B"], u)
                    tokens_out("A", "A.AO", x1, xb["A"], i)
                    dve.wait_ge(tokens["A"], u + 1)
                    free("A.AO")

            def free(name):
                nc.vector.nop().then_inc(pj_free[pj_bank(name)], 1)

            def high_h(m, i):
                u = unit("M", i)
                if not isinstance(i, int) or u:
                    dve.wait_ge(pj_full[pj_bank("M.Y1")], pj_use("M.Y1", i - 1))
                dve.wait_ge(pj_free[pj_bank(f"M.H{m}")], pj_use(f"M.H{m}", i))
                nc.vector.tensor_copy(h_hi[:, 2 * m:2 * m + 2, :], g[:, m, :, :]).then_inc(h_hi_done, 1)

            run(dve, body, 0, LAST)

        @block.gpsimd
        def _(pool):
            nc.gpsimd.memset(eps[:, :], EPS)
            nc.gpsimd.memset(half[:, :], -0.5).then_inc(half_set, 1)
            pool.wait_ge(const_in, CONST)
            nc.gpsimd.memset(bias_in[:, 16:20], 0.0).then_inc(setup_pool, 1)
            pool.wait_ge(half_set, 2)
            pool.wait_ge(masks_done, 2)

            def rstds(l, i, stage):
                n, u = LN[l], unit(stage, i)
                pool.wait_ge(ln_mv[l], u + 1)
                nc.gpsimd.tensor_tensor(veps[:, n, :], mv[:, n, :, 1], eps[:, :], ALU.add).then_inc(ln_eps[l], 1)
                pool.wait_ge(ln_eps[l], u + 1)
                nc.gpsimd.tensor_tensor(rstd[:, n, :], veps[:, n, :], half[:, :], ALU.pow).then_inc(ln_rstd[l], 1)

            def residual(stage, src, k, u):
                nc.gpsimd.tensor_tensor(xb[stage][:, :, :], src[:, :, :],
                                        brow[:, k, :].unsqueeze(1).broadcast_to([P, T, H]),
                                        ALU.add).then_inc(xb_done[stage], 1)

            def add_offset(a, i):
                u = unit(a, i)
                for r in range(R):
                    pool.wait_ge(masked[a], R * u + r + 1)
                    p3 = prob[a][:, r, :, :]
                    nc.gpsimd.tensor_tensor(p3, p3, of_tile(maskA_off if a == "A" else maskB_off, a, r),
                                            ALU.add).then_inc(offset[a], 1)

            def shift(a, i):
                u = unit(a, i)
                for r in range(R):
                    pool.wait_ge(maxed[a], R * u + r + 1)
                    p3 = prob[a][:, r, :, :].rearrange("p n (b k) -> p (n b) k", b=TILE)
                    nc.gpsimd.tensor_tensor(p3, p3, rmax[a][:, r, :].unsqueeze(2).broadcast_to(
                        [P, BL * TILE, S]), ALU.subtract).then_inc(shifted[a], 1)

            def low_h(m, i):
                u = unit("M", i)
                pool.wait_ge(h_hi_done, GELU * u + m + 1)
                nc.gpsimd.tensor_tensor(h_lo[:, 2 * m:2 * m + 2, :], g[:, m, :, :],
                                        h_hi[:, 2 * m:2 * m + 2, :].bitcast(F32), ALU.subtract).then_inc(h_lo_done, 1)

            def body(i):
                if active("B", i):
                    rstds("B", i, "B")
                    residual("B", x1, 1, unit("B", i))
                if active("A", i):
                    residual("A", x_in, 0, unit("A", i))
                if active("C", i):
                    shift("C", i)
                if active("M", i):
                    rstds("C", i, "M")
                if active("B", i):
                    pool.wait_ge(maskb_off_s, unit("B", i) + 1)
                    add_offset("B", i)
                if active("P", i):
                    rstds("A", i, "P")
                if active("B", i):
                    shift("B", i)
                if active("M", i):
                    for m in range(GELU):
                        low_h(m, i)
                if active("A", i):
                    add_offset("A", i)
                    shift("A", i)
                if active("B", i):
                    rstds("M", i, "B")
                    if active("M", i):
                        pool.wait_ge(tokens["M"], T * (unit("M", i) + 1))
                    residual("M", x2, 2, unit("B", i))

            run(pool, body, 0, LAST)


CONST = 16 * (2 + 3 + 3 + 1 + 2 * TILE)


def kernel(**inputs):
    import numpy as np
    import concourse.bacc as bacc
    from concourse.bass_utils import run_bass_kernel_spmd

    a = {k: np.asarray(v) for k, v in inputs.items()}
    L0, L1 = "L0_xattn_", "L1_xattn_"

    def by_parity(w):
        v = w.reshape(KC, HALVES, 2, 2, HD, *w.shape[1:])
        return v.transpose(3, 1, 0, 2, 4, *range(5, v.ndim)).reshape(w.shape)

    def columns(vectors):
        return np.concatenate(vectors).reshape(-1, P).T

    feature = np.arange(P)
    arrays = {
        "x": a["x"], "ctx_2048": a["ctx_2048"], "mask_1x1xSxS2_fc1": a["mask_1x1xSxS2_fc1"],
        "mask_Bx1xSxS2_ff1": a["mask_Bx1xSxS2_ff1"], "mask_BxS2_bf1": a["mask_BxS2_bf1"],
        "identity": np.eye(P, dtype=np.float32),
        "parity": np.stack([feature // n % 2 == e for n in (HD, 2 * HD) for e in range(2)], 1).astype(np.float32),
        "w_A_qkv": np.concatenate([a[L0 + "w_qkv"][:, :2 * H], by_parity(a[L0 + "w_qkv"][:, 2 * H:].T).T], 1),
        "w_A_o": by_parity(a[L0 + "w_ao"]),
        "w_B_q": a[L0 + "w_q"],
        "w_B_kv": np.concatenate([a[L0 + "w_kv"][:, :H], by_parity(a[L0 + "w_kv"][:, H:].T).T], 1),
        "w_B_o": by_parity(a[L0 + "w_co"]),
        "ln_vectors": columns([a[L0 + "ln1_s"], a[L0 + "ln1_b"], a[L0 + "ln2_s"], a[L0 + "ln2_b"],
                               a[L0 + "ln3_s"], a[L0 + "ln3_b"], a[L1 + "ln_gamma"], a[L1 + "ln_beta"]]),
        "biases": columns([a[L0 + "b_qkv"][:2 * H], by_parity(a[L0 + "b_qkv"][2 * H:]), a[L0 + "b_q"],
                           a[L0 + "b1"], a[L0 + "b_kv"][:H], by_parity(a[L0 + "b_kv"][H:])]),
        "w_M_1": a[L0 + "w1"], "w_M_2": a[L0 + "w2"],
        "w_C_q": a[L1 + "Wq"].T, "w_C_k": a[L1 + "Wk"].T, "w_C_v": by_parity(a[L1 + "Wv"]).T,
        "w_C_o": by_parity(a[L1 + "Wo"].T),
    }
    for n in ("b2", "b_ao", "b_co"):
        arrays[L0 + n] = a[L0 + n]
    arrays[L1 + "gate"] = a[L1 + "gate"]
    nc = bacc.Bacc("TRN2", target_bir_lowering=False, num_devices=1)
    arrays = {k: np.ascontiguousarray(v) for k, v in arrays.items()}
    d = {k: nc.dram_tensor("in_" + k, v.shape, mybir.dt.from_np(v.dtype), kind="ExternalInput").ap()
         for k, v in arrays.items()}
    out = nc.dram_tensor("out", (NB, S, H), F32, kind="ExternalOutput").ap()
    build(nc, d, out)
    r = run_bass_kernel_spmd(nc, [{"in_" + k: v for k, v in arrays.items()}], core_ids=[0])
    return r.results[0]["out"]
```

```python
from contextlib import ExitStack

import concourse.bass as bass
from concourse import mybir

F32 = mybir.dt.float32
F32R = mybir.dt.float32r
U8 = mybir.dt.uint8
ALU = mybir.AluOpType
ACT = mybir.ActivationFunctionType
AX = mybir.AxisListType

NB, S, H = 64, 64, 256
NH = 16
HD = H // NH
FF = 4 * H
P = 128
TILE = P // S
T = 2
UB = T * TILE
TOK = UB * S
U = NB // UB
KC = H // P
R = 4
BL = 4
NPAIR = NH // 2
HALVES = 2
VW = 2 * HD + 1
BANK = 512
EPS = 1e-5
OFF = 10000.0
FAR = 1e30

STAGES = "PABMC"
LAG = {s: n for n, s in enumerate(STAGES)}
FIRST = len(STAGES)
TAIL = len(STAGES) - 1
PJ = ["C.xT", "B.cT", "C.K", "C.Q", "M.zT", "A.zT", "B.V", "B.zT", "B.K", "B.Q", "M.H0", "M.H1",
      "M.H2", "A.K", "A.Q", "A.V", "M.H3", "C.OT", "M.cT", "C.AO", "M.Y0", "B.OT", "M.V", "B.AO",
      "A.OT", "M.Y1", "A.AO"]
PJ_BANKS = 4
S_USES = ["S_C", "S_B", "T_C", "S_A", "T_B", "T_A"]
ATT = "CBA"
GELU = 4


def unit(stage, i):
    return i - LAG[stage]


def active(stage, i):
    return not isinstance(i, int) or 0 <= unit(stage, i) < U


def starts(stage, i):
    return isinstance(i, int) and unit(stage, i) == 0


def pj_bank(name):
    return PJ.index(name) % PJ_BANKS


def pj_uses(b):
    return PJ[b::PJ_BANKS]


def pj_use(name, i):
    names = pj_uses(pj_bank(name))
    if isinstance(i, int):
        return sum(active(n[0], j) for j in range(i) for n in names) + sum(
            active(n[0], i) for n in names[:names.index(name) + 1])
    return pj_use(name, FIRST) + (i - FIRST) * len(names)


def score_use_before(use, i):
    k = S_USES.index(use)
    if not isinstance(i, int):
        n = S_USES[k - 1]
        return (n, unit(n[2], i) + 1) if k else (n, unit(n[2], i))
    done = [(n, unit(n[2], j) + 1) for j in range(i) for n in S_USES if active(n[2], j)]
    done += [(n, unit(n[2], i) + 1) for n in S_USES[:k] if active(n[2], i)]
    return done[-1] if done else None


def value_use(a, i):
    return ("M.V", i - 1) if a == "C" else (f"{a}.V", i)


def before(a, i):
    if not isinstance(i, int):
        n = ATT.index(a)
        return (ATT[n - 1], unit(ATT[n - 1], i) + 1) if n else (ATT[-1], unit(ATT[-1], i))
    done = [(x, unit(x, j) + 1) for j in range(i) for x in ATT if active(x, j)]
    done += [(x, unit(x, i) + 1) for x in ATT[:ATT.index(a)] if active(x, i)]
    return done[-1] if done else None


def build(nc, d, out):
    ctx = ExitStack()
    with ctx:
        def sb(name, shape, dt=F32):
            return ctx.enter_context(nc.sbuf_tensor(name, shape, dt))

        def ps(name):
            return ctx.enter_context(nc.psum_tensor(name, [P, BANK], F32))

        def sem(name):
            return ctx.enter_context(nc.semaphore(name))

        WCOLS = {"A_qkv": (3 * H, KC), "A_o": (H, KC), "B_q": (H, KC), "B_kv": (2 * H, KC),
                 "B_o": (H, KC), "M_1": (FF, KC), "M_2": (H, FF // P), "C_q": (H, KC),
                 "C_k": (H, KC), "C_v": (H, KC), "C_o": (H, KC)}
        w_hi = {n: sb(f"w_hi_{n}", [P, k, c], F32R) for n, (c, k) in WCOLS.items()}
        w_lo = {n: sb(f"w_lo_{n}", [P, k, c], F32R) for n, (c, k) in WCOLS.items()}

        consts = sb("consts", [P, sum(CONST_COLS)])
        at = [sum(CONST_COLS[:n]) for n in range(len(CONST_COLS) + 1)]
        ident, parity, lnvec, bias_in = (consts[:, at[n]:at[n + 1]] for n in range(len(CONST_COLS)))
        lnvec = lnvec.rearrange("p (n v k) -> p n v k", n=4, v=2)
        qscale = sb("qscale", [P, 2])
        bias = sb("bias", [P, CONST_COLS[-1]])
        BQ, BK, BV, BH = {"A": 0, "B": 6}, {"A": 2, "B": 20, "C": 16}, {"A": 4, "B": 22, "C": 18}, 8
        qbias = sb("qbias", [P, 2, 2, KC])
        kbias = sb("kbias", [P, 3, 2, KC])
        brow = sb("brow", [P, 3, H])
        gate = sb("gate", [P, 1])
        gate_t = sb("gate_t", [P, 1])
        half = sb("half", [P, T])
        eps = sb("eps", [P, T])
        maskA = sb("maskA", [P, TILE, S])
        maskA_off = sb("maskA_off", [P, TILE, S])

        x_in = sb("x_in", [P, T, H])
        ctx_b = sb("ctx_b", [P, T, H])
        ctx_c = sb("ctx_c", [P, T, H])
        z = {"A": sb("z_A", [P, T, H]), "B": sb("z_B", [P, T, H]), "M": sb("z_M", [P, T, H]),
             "C": ctx_c}
        xb = {s: sb(f"xb_{s}", [P, T, H]) for s in "ABM"}
        x1 = sb("x1", [P, T, H])
        x2 = sb("x2", [P, T, H])
        x3 = sb("x3", [P, T, H])
        y = sb("y", [P, T, H])
        stats = sb("stats", [P, 4, T, 6])
        mv = sb("mv", [P, 4, T, 2])
        veps = sb("veps", [P, 4, T])
        rstd = sb("rstd", [P, 4, T])
        maskB = sb("maskB", [P, UB, S])
        maskB_off = sb("maskB_off", [P, UB, S])
        maskC = sb("maskC", [P, UB, S], U8)
        maskC_off = sb("maskC_off", [P, UB, S])
        op = {k: (sb(f"{k}_hi", [P, KC, TOK], F32R), sb(f"{k}_lo", [P, KC, TOK], F32R))
              for k in ("zT_A", "zT_B", "cT_C", "xT_C", "cT_B", "zT_M", "oT")}
        OP = {"A.zT": op["zT_A"], "M.cT": op["cT_C"], "B.zT": op["zT_B"],
              "B.cT": op["cT_B"], "C.xT": op["xT_C"], "M.zT": op["zT_M"],
              "A.OT": op["oT"], "B.OT": op["oT"], "C.OT": op["oT"]}
        q2 = sb("q2", [P, KC, UB, 2, S])
        k2 = sb("k2", [P, KC, UB, 2, S])
        vz = {a: sb(f"vz_{a}", [P, T, NPAIR, TILE, VW]) for a in "ABC"}
        prob = {"B": sb("prob_B", [P, R, BL, TILE * S]),
                "A": sb("prob_AC", [P, R, BL, TILE * S])}
        prob["C"] = prob["A"]
        rmax = {a: sb(f"rmax_{a}", [P, R, BL * TILE]) for a in "ABC"}
        rden = {a: sb(f"rden_{a}", [P, R, BL * TILE]) for a in "ABC"}
        o = sb("o", [P, UB, NPAIR, HD])
        g = sb("g", [P, GELU, 2, TOK])
        h_hi = sb("h_hi", [P, FF // P, TOK], F32R)
        h_lo = sb("h_lo", [P, FF // P, TOK], F32R)

        s_bank = [ps(f"s_bank{r}") for r in range(R)]
        pj = [ps(f"pj{n}") for n in range(PJ_BANKS)]

        const_in, rest_in = sem("const_in"), sem("rest_in")
        weights_in = [sem(f"weights_in{n}") for n in range(5)]
        carried, setup_hi, setup_lo = sem("carried"), sem("setup_hi"), sem("setup_lo")
        bias_sum, bias_done, gate_done, masks_done = (sem(n) for n in ("bias_sum", "bias_done", "gate_done", "masks_done"))
        exponents_set, zeroed, ones_set = sem("exponents_set"), sem("zeroed"), sem("ones_set")
        x_in_s, ctxb_s, ctxc_s, maskb_s, maskc_s = (sem(n) for n in ("x_in_s", "ctxb_s", "ctxc_s", "maskb_s", "maskc_s"))
        pj_full = [sem(f"pj_full{n}") for n in range(PJ_BANKS)]
        pj_free = [sem(f"pj_free{n}") for n in range(PJ_BANKS)]
        hi_done = {n: sem("hi_" + n.replace(".", "_")) for n in OP}
        scored = {a: sem(f"scored_{a}") for a in "ABC"}
        masked = {a: sem(f"masked_{a}") for a in "ABC"}
        offset = {a: sem(f"offset_{a}") for a in "AB"}
        maxed = {a: sem(f"maxed_{a}") for a in "ABC"}
        shifted = {a: sem(f"shifted_{a}") for a in "ABC"}
        exped = {a: sem(f"exped_{a}") for a in "ABC"}
        turned = {a: sem(f"turned_{a}") for a in "ABC"}
        turned_in = {a: sem(f"turned_in_{a}") for a in "ABC"}
        summed = {a: sem(f"summed_{a}") for a in "ABC"}
        inverted = {a: sem(f"inverted_{a}") for a in "ABC"}
        normed = {a: sem(f"normed_{a}") for a in "ABC"}
        h_hi_done, h_lo_done = sem("h_hi_done"), sem("h_lo_done")
        tokens = {s: sem(f"tokens_{s}") for s in "ABMC"}
        ln_stats = {s: sem(f"ln_stats_{s}") for s in "ABMC"}
        ln_mv = {s: sem(f"ln_mv_{s}") for s in "ABMC"}
        ln_eps = {s: sem(f"ln_eps_{s}") for s in "ABMC"}
        ln_rstd = {s: sem(f"ln_rstd_{s}") for s in "ABMC"}
        ln_done = {s: sem(f"ln_done_{s}") for s in "ABMC"}
        xb_done = {s: sem(f"xb_done_{s}") for s in "ABM"}
        maskb_off_s, maskc_off_s = sem("maskb_off_s"), sem("maskc_off_s")
        stored = sem("stored")

        LN = {"A": 0, "B": 1, "M": 2, "C": 3}

        x_d = d["x"].rearrange("(u t b) s c -> u (b s) t c", t=T, b=TILE)
        c_d = d["ctx_2048"].rearrange("(u t b) s c -> u (b s) t c", t=T, b=TILE)
        y_d = out.rearrange("(u t b) s c -> u (b s) t c", t=T, b=TILE)
        mB_d = d["mask_Bx1xSxS2_ff1"].rearrange("(u b) o q k -> u (o q) b k", b=UB)
        mC_d = d["mask_BxS2_bf1"].rearrange("(u o b) k -> u o (b k)", b=UB, o=1)

        def rows(name):
            return d[name].rearrange("(k p) c -> p k c", p=P)

        def flat(t):
            return t.rearrange("p a b c -> p (a b c)")

        bufA, bufB, bufM = flat(prob["A"][:, :, :, :]), flat(prob["B"][:, :, :, :]), flat(g[:, :, :, :])
        bufx, bufy = (t[:, :, :].rearrange("p a b -> p (a b)") for t in (x3, y))
        BATCHES = [[("A_qkv", "A", bufA, 0), ("A_o", None, bufA, 6 * H)],
                   [("B_q", "B", bufB, 0), ("B_kv", None, bufB, 2 * H), ("B_o", None, bufB, 6 * H)],
                   [("M_1", "M", bufM, 0)],
                   [("C_v", "C", bufx, 0), ("C_k", "C", bufy, 0)],
                   [("M_2", None, bufM, 0), ("C_q", None, bufx, 0), ("C_o", "gate", bufy, 0)]]
        pieces = []
        for batch, names in enumerate(BATCHES):
            for name, scaled, buf, at in names:
                c, k = WCOLS[name]
                pieces.append((batch, name, scaled, buf[:, at:at + k * c].rearrange("p (k c) -> p k c", k=k), k))

        def pieces_until(batch):
            return sum(len(b) for b in BATCHES[:batch + 1])

        def row_scale(scaled, k):
            return gate_t[:, 0:1] if scaled == "gate" else lnvec[:, LN[scaled], 0, k:k + 1]

        def of_tile(m, a, r):
            t = r // HALVES
            m = m[:, :, :] if a == "A" else m[:, t * TILE:(t + 1) * TILE, :]
            return m.rearrange("p b k -> p (b k)").unsqueeze(1).broadcast_to([P, BL, TILE * S])

        block = ctx.enter_context(nc.Block())

        FEATURE = {"A.Q": ("A.zT", "A_qkv", 0), "A.K": ("A.zT", "A_qkv", H),
                   "B.Q": ("B.zT", "B_q", 0), "B.K": ("B.cT", "B_kv", 0),
                   "C.Q": ("C.xT", "C_q", 0), "C.K": ("M.cT", "C_k", 0),
                   **{f"M.H{m}": ("M.zT", "M_1", m * 2 * P) for m in range(GELU)}}
        TOKEN = {"A.V": ("A.zT", "A_qkv", 2 * H), "B.V": ("B.cT", "B_kv", H), "M.V": ("M.cT", "C_v", 0),
                 "A.AO": ("A.OT", "A_o", 0), "B.AO": ("B.OT", "B_o", 0), "C.AO": ("C.OT", "C_o", 0)}

        def run(eng, body, first, last):
            for i in range(first, min(FIRST, last + 1)):
                body(i)
            with eng.Fori(FIRST, U) as i:
                body(i)
            for i in range(U, last + 1):
                body(i)

        LAST = U - 1 + TAIL

        @block.sync
        def _(sp):
            def rest(dst, src):
                sp.dma_start(dst, src).then_inc(rest_in, 16)

            def load(batch):
                for b, name, scaled, dst, kc in pieces:
                    if b == batch:
                        sp.dma_start(dst, rows("w_" + name)).then_inc(weights_in[batch], 16)

            def value(x):
                return x if isinstance(x, int) else sp.snap(x)

            def tokens_in(i):
                if active("P", i):
                    u = unit("P", i)
                    if not isinstance(i, int) or u:
                        sp.wait_ge(ln_done["A"], u)
                        sp.wait_ge(xb_done["A"], u)
                    sp.dma_start(x_in[:, :, :], x_d[i]).then_inc(x_in_s, 16)

            def body(i):
                later = not isinstance(i, int)
                b_masked = value(R * unit("B", i))
                u_b, u_m, c_out = value(unit("B", i)), value(unit("M", i)), value(unit("C", i) + 1)
                if active("B", i):
                    u = u_b
                    if later or u:
                        sp.wait_ge(hi_done["B.cT"], u)
                    sp.dma_start(ctx_b[:, :, :], c_d[u]).then_inc(ctxb_s, 16)
                    if later or u:
                        sp.wait_ge(masked["B"], b_masked)
                        sp.wait_ge(maskb_off_s, u)
                    for hp in range(2):
                        sp.dma_start(maskB[hp * S:(hp + 1) * S, :, :], mB_d[u]).then_inc(maskb_s, 16)
                if active("M", i):
                    u = u_m
                    if later or u:
                        sp.wait_ge(maskc_off_s, u)
                        sp.wait_ge(hi_done["M.cT"], u)
                    sp.dma_start(ctx_c[:, :, :], c_d[u]).then_inc(ctxc_s, 16)
                    sp.dma_start(maskC[:, :, :].rearrange("p b k -> p (b k)"),
                                 mC_d[u].broadcast_to([P, UB * S])).then_inc(maskc_s, 16)
                tokens_in(i)
                if active("C", i):
                    sp.wait_ge(tokens["C"], c_out)
                    sp.dma_start(y_d[unit("C", i)], y[:, :, :]).then_inc(stored, 16)

            sp.dma_start(consts[:, :], d["constants"]).then_inc(const_in, 16)
            load(0)
            body(0)
            rest(brow[:, :, :].rearrange("p v c -> p (v c)"), d["rows"].broadcast_to([P, 3 * H]))
            for hp in range(2):
                mask = d["mask_1x1xSxS2_fc1"].rearrange("o q s k -> (o s) q k")
                rest(maskA[hp * S:(hp + 1) * S, :, :], mask.broadcast_to([S, TILE, S]))
            rest(gate[:, :], d["L1_xattn_gate"].rearrange("(o c) -> o c", o=1).broadcast_to([P, 1]))
            load(1)
            load(2)
            load(3)
            body(1)
            body(2)
            sp.wait_ge(setup_lo, pieces_until(3))
            load(4)
            run(sp, body, 3, LAST)
            sp.wait_ge(stored, 16 * U)

        @block.tensor
        def _(pe):
            def carry_shifts(batches, bank):
                for batch, name, scaled, w, kc in pieces:
                    if batch not in batches or scaled not in LN:
                        continue
                    pe.wait_ge(weights_in[batch], 16 * len(BATCHES[batch]))
                    shift = lnvec[:, LN[scaled], 1, :]
                    cols = WCOLS[name][0]
                    at = {"A_qkv": 0, "B_q": 6, "M_1": 8, "C_k": 16, "C_v": 18}[name]
                    for m in range(cols // P):
                        for k in range(KC):
                            last = nc.tensor.matmul(pj[bank][:, at + m:at + m + 1], w[:, k, m * P:(m + 1) * P],
                                                    shift[:, k:k + 1], start=(k == 0), stop=(k == KC - 1))
                last.then_inc(carried, 1)

            def wait_weights(batch):
                pe.wait_ge(setup_lo, pieces_until(batch))

            def claim(name, i):
                n = pj_use(name, i) - 1
                if not isinstance(n, int) or n:
                    pe.wait_ge(pj_free[pj_bank(name)], n)
                return pj[pj_bank(name)]

            def turn(name, src, i):
                bank = claim(name, i)
                for k in range(KC):
                    for t in range(T):
                        at = k * TOK + t * P
                        last = nc.tensor.transpose(bank[:, at:at + P], src[:, t, k * P:(k + 1) * P], ident[:, :])
                last.then_inc(pj_full[pj_bank(name)], 1)

            def parts(x, w):
                return ((x[0], w_hi[w]), (x[1], w_hi[w]), (x[0], w_lo[w]))

            def feature_major(name, i):
                src, w, col = FEATURE[name]
                j = i - 1 if (name, src) == ("C.K", "M.cT") else i
                pe.wait_ge(pj_free[pj_bank(src)], pj_use(src, j))
                bank = claim(name, i)
                for m in range(2):
                    n = 0
                    for k in range(KC):
                        for x, wt in parts(OP[src], w):
                            last = nc.tensor.matmul(bank[:, m * TOK:(m + 1) * TOK],
                                                    wt[:, k, col + m * P:col + (m + 1) * P], x[:, k, :],
                                                    start=(n == 0), stop=(n == 3 * KC - 1))
                            n += 1
                last.then_inc(pj_full[pj_bank(name)], 1)

            def token_major(name, i):
                src, w, col = TOKEN[name]
                pe.wait_ge(pj_free[pj_bank(src)], pj_use(src, i))
                bank = claim(name, i)
                for t in range(T):
                    n = 0
                    for k in range(KC):
                        for x, wt in parts(OP[src], w):
                            last = nc.tensor.matmul(bank[:, t * H:(t + 1) * H], x[:, k, t * P:(t + 1) * P],
                                                    wt[:, k, col:col + H],
                                                    start=(n == 0), stop=(n == 3 * KC - 1))
                            n += 1
                last.then_inc(pj_full[pj_bank(name)], 1)

            def mlp_out(t, i):
                u = unit("M", i)
                pe.wait_ge(h_lo_done, GELU * (u + 1))
                bank = claim(f"M.Y{t}", i)
                n = 0
                for k in range(FF // P):
                    for x, wt in ((h_hi, w_hi["M_2"]), (h_lo, w_hi["M_2"]), (h_hi, w_lo["M_2"])):
                        last = nc.tensor.matmul(bank[:, 0:H], x[:, k, t * P:(t + 1) * P],
                                                wt[:, k, :], start=(n == 0), stop=(n == 3 * (FF // P) - 1))
                        n += 1
                last.then_inc(pj_full[pj_bank(f"M.Y{t}")], 1)

            def wait_score_banks(use, i, r):
                if b := score_use_before(use, i):
                    read = masked if b[0][0] == "S" else normed
                    pe.wait_ge(read[b[0][2]], R * (b[1] - 1) + r + 1)

            def scores(a, i):
                for name in (f"{a}.Q", f"{a}.K"):
                    pe.wait_ge(pj_free[pj_bank(name)], pj_use(name, i))
                for t in range(T):
                    wait_score_banks(f"S_{a}", i, HALVES * (t + 1) - 1)
                    for c in range(KC):
                        for b2 in range(TILE):
                            for half in range(HALVES):
                                rows_ = slice(half * S, (half + 1) * S)
                                bank = s_bank[t * HALVES + half][:, :].rearrange(
                                    "p (c s b k) -> p c s b k", c=KC, s=2, b=TILE)
                                mm = nc.tensor.matmul(bank[:, c, :, b2, :],
                                                      q2[rows_, c, t * TILE + b2].rearrange("p e q -> p (e q)"),
                                                      k2[rows_, c, t * TILE + b2], start=True, stop=True)
                                if (c, b2) == (KC - 1, TILE - 1):
                                    mm.then_inc(scored[a], 1)

            def turn_probs(a, r, i):
                wait_score_banks(f"T_{a}", i, r)
                pe.wait_ge(exped[a], R * unit(a, i) + r + 1)
                for n in range(BL):
                    last = nc.tensor.transpose(s_bank[r][:, n * P:(n + 1) * P], prob[a][:, r, n, :], ident[:, :])
                last.then_inc(turned[a], 1)

            def values(a, r, i):
                u = unit(a, i)
                if r == 0:
                    name, j = value_use(a, i)
                    pe.wait_ge(pj_free[pj_bank(name)], pj_use(name, j))
                pe.wait_ge(turned_in[a], R * u + r + 1)
                t, half = divmod(r, HALVES)
                for n in range(BL):
                    last = nc.tensor.matmul(s_bank[r][:, n * TILE * VW:(n + 1) * TILE * VW],
                                            prob[a][:, r, n, :], vz[a][:, t, half * BL + n, :, :],
                                            start=True, stop=True)
                last.then_inc(summed[a], 1)

            def attend(a, i):
                for r in range(R):
                    turn_probs(a, r, i)
                for r in range(R):
                    values(a, r, i)

            def turn_out(a, i):
                name = f"{a}.OT"
                pe.wait_ge(normed[a], R * (unit(a, i) + 1))
                bank = claim(name, i)
                for b in range(UB):
                    last = nc.tensor.transpose(bank[:, b * P:(b + 1) * P],
                                               o[:, b].rearrange("p m f -> p (m f)"), ident[:, :])
                last.then_inc(pj_full[pj_bank(name)], 1)

            def body(i):
                if active("C", i):
                    pe.wait_ge(tokens["M"], T * (unit("C", i) + 1))
                    turn("C.xT", x3, i)
                if active("B", i):
                    pe.wait_ge(ctxb_s, 16 * (unit("B", i) + 1))
                    turn("B.cT", ctx_b, i)
                if active("C", i):
                    feature_major("C.K", i)
                    feature_major("C.Q", i)
                if active("M", i):
                    pe.wait_ge(ln_done["M"], unit("M", i) + 1)
                    turn("M.zT", z["M"], i)
                if active("A", i):
                    pe.wait_ge(ln_done["A"], unit("A", i) + 1)
                    turn("A.zT", z["A"], i)
                if active("B", i):
                    if starts("B", i):
                        wait_weights(1)
                        pe.wait_ge(bias_done, 3)
                    token_major("B.V", i)
                    pe.wait_ge(ln_done["B"], unit("B", i) + 1)
                    turn("B.zT", z["B"], i)
                if active("C", i):
                    scores("C", i)
                if active("B", i):
                    feature_major("B.K", i)
                    feature_major("B.Q", i)
                if active("M", i):
                    if starts("M", i):
                        wait_weights(2)
                    feature_major("M.H0", i)
                    feature_major("M.H1", i)
                if active("B", i):
                    scores("B", i)
                if active("M", i):
                    feature_major("M.H2", i)
                if active("C", i):
                    attend("C", i)
                if active("A", i):
                    if starts("A", i):
                        wait_weights(0)
                        pe.wait_ge(bias_done, 1)
                    feature_major("A.K", i)
                    feature_major("A.Q", i)
                    token_major("A.V", i)
                if active("M", i):
                    feature_major("M.H3", i)
                if active("C", i):
                    turn_out("C", i)
                if active("M", i):
                    pe.wait_ge(ln_done["C"], unit("M", i) + 1)
                    turn("M.cT", ctx_c, i)
                if active("A", i):
                    scores("A", i)
                    if starts("A", i):
                        carry_shifts((1, 2), pj_bank("A.OT"))
                if active("C", i):
                    token_major("C.AO", i)
                if active("B", i):
                    attend("B", i)
                if active("M", i):
                    if starts("M", i):
                        wait_weights(4)
                    mlp_out(0, i)
                if active("B", i):
                    turn_out("B", i)
                if active("M", i):
                    token_major("M.V", i)
                if active("A", i):
                    attend("A", i)
                if active("B", i):
                    token_major("B.AO", i)
                if active("A", i):
                    if starts("A", i):
                        pe.wait_ge(bias_done, 2)
                    turn_out("A", i)
                    if starts("A", i):
                        carry_shifts((3,), pj_bank("A.V"))
                if active("M", i):
                    mlp_out(1, i)
                if active("A", i):
                    token_major("A.AO", i)

            pe.wait_ge(const_in, 16)
            carry_shifts((0,), pj_bank("A.OT"))
            run(pe, body, 1, LAST)

        @block.scalar
        def _(act):
            act.wait_ge(const_in, 16)

            def high_weights(batches):
                for batch, name, scaled, w, kc in pieces:
                    if batch not in batches:
                        continue
                    act.wait_ge(weights_in[batch], 16 * len(BATCHES[batch]))
                    if scaled:
                        for k in range(kc):
                            last = nc.scalar.activation(w_hi[name][:, k, :], w[:, k, :], ACT.Copy,
                                                        scale=row_scale(scaled, k))
                    else:
                        last = nc.scalar.activation(w_hi[name][:, :, :], w, ACT.Copy)
                    last.then_inc(setup_hi, 1)

            high_weights((0,))
            act.wait_ge(rest_in, REST)
            nc.scalar.activation(gate_t[:, :], gate[:, :], ACT.Tanh).then_inc(gate_done, 1)
            act.wait_ge(gate_done, 1)

            def high_part(name, i, used_by=None, bias_cols=None):
                if used_by and (not isinstance(i, int) or pj_use(used_by[0], used_by[1])):
                    act.wait_ge(pj_full[pj_bank(used_by[0])], pj_use(used_by[0], used_by[1]))
                act.wait_ge(pj_full[pj_bank(name)], pj_use(name, i))
                bank = pj[pj_bank(name)]
                hi = OP[name][0]
                if bias_cols is None:
                    last = nc.scalar.activation(hi[:, :, :].rearrange("p k t -> p (k t)"), bank[:, :], ACT.Copy)
                else:
                    turned_o = bank[:, :].rearrange("p (b e q) -> p e b q", b=UB, e=2)
                    for e in range(KC):
                        last = nc.scalar.activation(hi[:, e, :].rearrange("p (b q) -> p b q", b=UB), turned_o[:, e],
                                                    ACT.Identity, bias=bias[:, bias_cols + e:bias_cols + e + 1])
                last.then_inc(hi_done[name], 1)

            def wait_scores_before(a, i):
                if b := before(a, i):
                    act.wait_ge(scored[b[0]], R * b[1])

            def queries(a, i):
                name = f"{a}.Q"
                act.wait_ge(pj_full[pj_bank(name)], pj_use(name, i))
                q_all = pj[pj_bank(name)][:, :].rearrange("p (m b q) -> p m b q", m=KC, b=UB)
                for e in range(2):
                    if a == "C":
                        last = nc.scalar.activation(q2[:, :, :, e, :], q_all, ACT.Copy, scale=qscale[:, e:e + 1])
                    else:
                        for m in range(KC):
                            last = nc.scalar.activation(q2[:, m, :, e, :], q_all[:, m], ACT.Identity,
                                                        bias=qbias[:, "AB".index(a), e, m:m + 1],
                                                        scale=qscale[:, e:e + 1])
                last.then_inc(pj_free[pj_bank(name)], 1)

            def keys(a, i):
                name = f"{a}.K"
                wait_scores_before(a, i)
                act.wait_ge(pj_full[pj_bank(name)], pj_use(name, i))
                k_all = pj[pj_bank(name)][:, :].rearrange("p (m b k) -> p m b k", m=KC, b=UB)
                for s in range(2):
                    for m in range(KC):
                        last = nc.scalar.activation(k2[:, m, :, s, :], k_all[:, m], ACT.Identity,
                                                    bias=kbias[:, "ABC".index(a), s, m:m + 1],
                                                    scale=parity[:, 2 + s:3 + s])
                last.then_inc(pj_free[pj_bank(name)], 1)

            def exps(a, i):
                for r in range(R):
                    act.wait_ge(shifted[a], R * unit(a, i) + r + 1)
                    p2 = prob[a][:, r, :, :].rearrange("p n k -> p (n k)")
                    nc.scalar.activation(p2, p2, ACT.Exp).then_inc(exped[a], 1)

            def turned_back(a, i):
                for r in range(R):
                    act.wait_ge(turned[a], R * unit(a, i) + r + 1)
                    nc.scalar.activation(prob[a][:, r, :, :].rearrange("p n k -> p (n k)"), s_bank[r][:, :],
                                         ACT.Copy).then_inc(turned_in[a], 1)

            def gelus(m, i):
                name = f"M.H{m}"
                u = unit("M", i)
                act.wait_ge(pj_full[pj_bank(name)], pj_use(name, i))
                if not isinstance(i, int) or u:
                    act.wait_ge(h_lo_done, GELU * (u - 1) + m + 1)
                bank = pj[pj_bank(name)]
                for k in range(2):
                    c = BH + 2 * m + k
                    last = nc.scalar.activation(g[:, m, k, :], bank[:, k * TOK:(k + 1) * TOK],
                                                ACT.Gelu_apprx_tanh, bias=bias[:, c:c + 1])
                last.then_inc(pj_free[pj_bank(name)], 1)

            def body(i):
                if active("C", i):
                    high_part("C.xT", i, ("C.Q", i - 1))
                if active("B", i):
                    high_part("B.cT", i, ("B.K", i - 1))
                if active("C", i):
                    keys("C", i)
                    queries("C", i)
                if active("M", i):
                    high_part("M.zT", i, ("M.H3", i - 1))
                if active("A", i):
                    high_part("A.zT", i, ("A.V", i - 1))
                if active("B", i):
                    high_part("B.zT", i, ("B.Q", i - 1))
                    keys("B", i)
                    queries("B", i)
                if active("C", i) and active("B", i):
                    exps("C", i)
                if active("M", i):
                    if starts("M", i):
                        act.wait_ge(setup_lo, pieces_until(4))
                    for m in range(GELU - 1):
                        gelus(m, i)
                if active("C", i):
                    if not active("B", i):
                        exps("C", i)
                    turned_back("C", i)
                if active("A", i):
                    keys("A", i)
                    queries("A", i)
                if active("M", i):
                    gelus(GELU - 1, i)
                if active("C", i):
                    high_part("C.OT", i, ("A.AO", i - 1), BV["C"])
                if active("M", i):
                    high_part("M.cT", i, ("C.K", i))
                if active("B", i):
                    exps("B", i)
                    turned_back("B", i)
                if active("A", i):
                    exps("A", i)
                if active("B", i):
                    high_part("B.OT", i, ("C.AO", i), BV["B"])
                if active("A", i):
                    turned_back("A", i)
                    if starts("A", i):
                        high_weights((1, 2))
                    high_part("A.OT", i, ("B.AO", i), BV["A"])
                    if starts("A", i):
                        high_weights((3,))
                    if starts("B", i):
                        high_weights((4,))

            run(act, body, 1, LAST)

        @block.vector
        def _(dve):
            for a in "ABC":
                last = nc.vector.memset(vz[a][:, :, :, :, :], 0.0)
            last.then_inc(zeroed, 1)
            dve.wait_ge(zeroed, 1)
            for a in "ABC":
                for b2 in range(TILE):
                    last = nc.vector.memset(vz[a][b2 * S:(b2 + 1) * S, :, :, b2, 2 * HD:VW], 1.0)
            last.then_inc(ones_set, 1)
            dve.wait_ge(const_in, 16)
            nc.vector.tensor_scalar(qscale[:, :], parity[:, 0:2], HD ** -0.5, None, ALU.mult).then_inc(masks_done, 1)
            dve.wait_ge(masks_done, 1)

            def low_weights(batch):
                for n, (b, name, scaled, w, kc) in enumerate(pieces):
                    if b != batch:
                        continue
                    dve.wait_ge(setup_hi, n + 1)
                    hi = w_hi[name][:, :, :].bitcast(F32)
                    if scaled:
                        for k in range(kc):
                            last = nc.vector.scalar_tensor_tensor(w_lo[name][:, k, :], w[:, k, :], row_scale(scaled, k),
                                                                  hi[:, k, :], ALU.mult, ALU.subtract)
                    else:
                        last = nc.vector.tensor_tensor(w_lo[name][:, :, :], w, hi, ALU.subtract)
                    last.then_inc(setup_lo, 1)

            def finish_biases(stage, done):
                dve.wait_ge(carried, done)
                c0, c1 = {"A": (0, 6), "B": (6, 16), "C": (16, 20)}[stage]
                bank = pj[pj_bank("A.V" if stage == "C" else "A.OT")]
                nc.vector.tensor_tensor(bias[:, c0:c1], bank[:, c0:c1], bias_in[:, c0:c1], ALU.add).then_inc(bias_sum, 1)
                if stage == "A":
                    nc.vector.tensor_copy(bias[:, 20:24], bias_in[:, 20:24]).then_inc(bias_sum, 1)
                dve.wait_ge(bias_sum, done + 1)
                for e in range(2):
                    if stage != "C":
                        nc.vector.tensor_scalar(qbias[:, "AB".index(stage), e, :], bias[:, BQ[stage]:BQ[stage] + KC],
                                                qscale[:, e:e + 1], None, ALU.mult)
                    last = nc.vector.tensor_scalar(kbias[:, "ABC".index(stage), e, :], bias[:, BK[stage]:BK[stage] + KC],
                                                   parity[:, 2 + e:3 + e], None, ALU.mult)
                last.then_inc(bias_done, 1)

            def low_part(name, i, bias_cols=None):
                dve.wait_ge(hi_done[name], unit(name[0], i) + 1)
                bank = pj[pj_bank(name)]
                hi, lo = OP[name]
                hi = hi[:, :, :].bitcast(F32)
                if bias_cols is None:
                    last = nc.vector.tensor_tensor(lo[:, :, :].rearrange("p k t -> p (k t)"), bank[:, :],
                                                   hi.rearrange("p k t -> p (k t)"), ALU.subtract)
                else:
                    turned_o = bank[:, :].rearrange("p (b e q) -> p e b q", b=UB, e=2)
                    for e in range(KC):
                        last = nc.vector.scalar_tensor_tensor(
                            lo[:, e, :].rearrange("p (b q) -> p b q", b=UB), turned_o[:, e],
                            bias[:, bias_cols + e:bias_cols + e + 1],
                            hi[:, e, :].rearrange("p (b q) -> p b q", b=UB), ALU.add, ALU.subtract)
                last.then_inc(pj_free[pj_bank(name)], 1)

            def value_rows(a, name, i):
                dve.wait_ge(pj_full[pj_bank(name)], pj_use(name, i))
                v = pj[pj_bank(name)][:, :].rearrange("p (t e m f) -> p t m e f", t=T, e=2, m=NPAIR)
                for t in range(T):
                    for b2 in range(TILE):
                        rows_ = slice(b2 * S, (b2 + 1) * S)
                        dst = vz[a][rows_, t, :, b2, 0:2 * HD].rearrange("p m (e f) -> p m e f", e=2)
                        last = nc.vector.tensor_copy(dst, v[rows_, t])
                last.then_inc(pj_free[pj_bank(name)], 1)

            def mask_scores(a, r, i):
                dve.wait_ge(scored[a], R * unit(a, i) + r + 1)
                m, f = {"A": (maskA, ALU.mult), "B": (maskB, ALU.mult), "C": (maskC_off, ALU.add)}[a]
                nc.vector.tensor_tensor(prob[a][:, r, :, :], s_bank[r][:, :].rearrange("p (n k) -> p n k", n=BL),
                                        of_tile(m, a, r), f).then_inc(masked[a], 1)

            def row_max(a, r, i):
                dve.wait_ge((masked if a == "C" else offset)[a], R * unit(a, i) + r + 1)
                nc.vector.tensor_reduce(rmax[a][:, r, :], prob[a][:, r, :, :].rearrange("p n (b k) -> p (n b) k", b=TILE),
                                        AX.X, ALU.max).then_inc(maxed[a], 1)

            def normalise(a, i, rs=range(R)):
                u = unit(a, i)
                for r in rs:
                    dve.wait_ge(summed[a], R * u + r + 1)
                    t, half = divmod(r, HALVES)
                    sums = s_bank[r][:, 0:BL * TILE * VW].rearrange("p (n v) -> p n v", v=VW)
                    nc.vector.reciprocal(rden[a][:, r, :], sums[:, :, 2 * HD]).then_inc(inverted[a], 1)
                    dve.wait_ge(inverted[a], R * u + r + 1)
                    for e in range(2):
                        rows_ = slice(e * S, (e + 1) * S)
                        last = nc.vector.tensor_tensor(
                            o[rows_, t * TILE:(t + 1) * TILE, half * BL:(half + 1) * BL, :],
                            sums[rows_, :, e * HD:(e + 1) * HD].rearrange("p (n b) f -> p b n f", b=TILE),
                            rden[a][rows_, r, :].rearrange("p (n b) -> p b n", b=TILE).unsqueeze(3).broadcast_to(
                                [S, TILE, BL, HD]), ALU.mult)
                    last.then_inc(normed[a], 1)

            def tokens_out(stage, bank_use, dst, residual, i):
                dve.wait_ge(pj_full[pj_bank(bank_use)], pj_use(bank_use, i))
                nc.vector.tensor_tensor(dst[:, :, :].rearrange("p t c -> p (t c)"), pj[pj_bank(bank_use)][:, :],
                                        residual[:, :, :].rearrange("p t c -> p (t c)"),
                                        ALU.add).then_inc(tokens[stage], 1)

            def mlp_tokens(t, i):
                name = f"M.Y{t}"
                dve.wait_ge(pj_full[pj_bank(name)], pj_use(name, i))
                nc.vector.tensor_tensor(x3[:, t, :], pj[pj_bank(name)][:, 0:H], xb["M"][:, t, :],
                                        ALU.add).then_inc(tokens["M"], 1)
                dve.wait_ge(tokens["M"], T * unit("M", i) + t + 1)
                free(name)

            def moments(l, src, u):
                n = LN[l]
                for t in range(T):
                    last = nc.vector.bn_stats(stats[:, n, t, :], src[:, t, :])
                last.then_inc(ln_stats[l], 1)
                dve.wait_ge(const_in, 16)
                dve.wait_ge(ln_stats[l], u + 1)
                for t in range(T):
                    last = nc.vector.bn_aggr(mv[:, n, t, :], stats[:, n, t, :])
                last.then_inc(ln_mv[l], 1)

            def normalised(l, src, u):
                n = LN[l]
                dve.wait_ge(ln_rstd[l], u + 1)
                for t in range(T):
                    last = nc.vector.tensor_scalar(z[l][:, t, :], src[:, t, :], mv[:, n, t, 0:1],
                                                   rstd[:, n, t:t + 1], ALU.subtract, ALU.mult)
                last.then_inc(ln_done[l], 1)

            def body(i):
                if starts("A", i):
                    dve.wait_ge(rest_in, REST)
                    nc.vector.tensor_scalar(maskA_off[:, :, :], maskA[:, :, :], 1.0, OFF, ALU.subtract,
                                            ALU.mult).then_inc(masks_done, 1)
                    dve.wait_ge(gate_done, 1)
                    low_weights(0)
                    finish_biases("A", 1)
                if active("C", i):
                    low_part("C.xT", i)
                if active("B", i):
                    low_part("B.cT", i)
                    dve.wait_ge(tokens["A"], unit("B", i) + 1)
                    moments("B", x1, unit("B", i))
                    normalised("B", x1, unit("B", i))
                if active("M", i):
                    low_part("M.zT", i)
                if active("A", i):
                    low_part("A.zT", i)
                if active("B", i):
                    low_part("B.zT", i)
                if active("C", i):
                    dve.wait_ge(maskc_off_s, unit("C", i) + 1)
                    for r in range(R):
                        mask_scores("C", r, i)
                        if r == 1 and not active("B", i):
                            row_max("C", 0, i)
                            row_max("C", 1, i)
                if active("B", i):
                    value_rows("B", "B.V", i)
                    if starts("B", i):
                        low_weights(2)
                        low_weights(3)
                    if starts("M", i):
                        low_weights(4)
                if active("C", i):
                    for r in range(0 if active("B", i) else 2, R):
                        row_max("C", r, i)
                if active("M", i):
                    u = unit("M", i)
                    dve.wait_ge(maskc_s, 16 * (u + 1))
                    nc.vector.tensor_scalar(maskC_off[:, :, :], maskC[:, :, :], 1.0, FAR, ALU.subtract,
                                            ALU.mult).then_inc(maskc_off_s, 1)
                    dve.wait_ge(ctxc_s, 16 * (u + 1))
                    moments("C", ctx_c, u)
                if active("B", i):
                    u = unit("B", i)
                    dve.wait_ge(maskb_s, 32 * (u + 1))
                    if not isinstance(i, int) or u:
                        dve.wait_ge(offset["B"], R * u)
                    nc.vector.tensor_scalar(maskB_off[:, :, :], maskB[:, :, :], 1.0, OFF, ALU.subtract,
                                            ALU.mult).then_inc(maskb_off_s, 1)
                    for r in range(R):
                        mask_scores("B", r, i)
                if active("P", i):
                    dve.wait_ge(x_in_s, 16 * (unit("P", i) + 1))
                    moments("A", x_in, unit("P", i))
                for n in range(R):
                    if active("B", i):
                        row_max("B", n, i)
                    if active("M", i) and n < GELU - 1:
                        high_h(n, i)
                if active("M", i):
                    normalised("C", ctx_c, unit("M", i))
                if active("C", i):
                    normalise("C", i)
                if active("P", i):
                    normalised("A", x_in, unit("P", i))
                if active("A", i):
                    value_rows("A", "A.V", i)
                if active("M", i):
                    high_h(GELU - 1, i)
                if active("C", i):
                    low_part("C.OT", i, BV["C"])
                if active("M", i):
                    low_part("M.cT", i)
                if active("A", i):
                    for r in range(R):
                        mask_scores("A", r, i)
                if active("C", i):
                    u = unit("C", i)
                    if not isinstance(i, int) or u:
                        dve.wait_ge(stored, 16 * u)
                    tokens_out("C", "C.AO", y, x3, i)
                    dve.wait_ge(tokens["C"], u + 1)
                    free("C.AO")
                for r in range(R):
                    if active("A", i):
                        row_max("A", r, i)
                    if active("B", i):
                        normalise("B", i, [r])
                if starts("A", i):
                    finish_biases("B", 2)
                if active("M", i):
                    dve.wait_ge(xb_done["M"], unit("M", i) + 1)
                    mlp_tokens(0, i)
                if active("B", i):
                    low_part("B.OT", i, BV["B"])
                if active("M", i):
                    value_rows("C", "M.V", i)
                if active("A", i):
                    normalise("A", i)
                if active("B", i):
                    u = unit("B", i)
                    dve.wait_ge(xb_done["B"], u + 1)
                    if not isinstance(i, int) or u:
                        dve.wait_ge(xb_done["M"], u)
                    tokens_out("B", "B.AO", x2, xb["B"], i)
                    dve.wait_ge(tokens["B"], u + 1)
                    free("B.AO")
                    moments("M", x2, u)
                if active("A", i):
                    low_part("A.OT", i, BV["A"])
                    if starts("A", i):
                        low_weights(1)
                        finish_biases("C", 3)
                if active("B", i):
                    normalised("M", x2, unit("B", i))
                if active("M", i):
                    mlp_tokens(1, i)
                if active("A", i):
                    u = unit("A", i)
                    dve.wait_ge(xb_done["A"], u + 1)
                    if not isinstance(i, int) or u:
                        dve.wait_ge(xb_done["B"], u)
                    tokens_out("A", "A.AO", x1, xb["A"], i)
                    dve.wait_ge(tokens["A"], u + 1)
                    free("A.AO")

            def free(name):
                nc.vector.nop().then_inc(pj_free[pj_bank(name)], 1)

            def high_h(m, i):
                u = unit("M", i)
                if not isinstance(i, int) or u:
                    dve.wait_ge(pj_full[pj_bank("M.Y1")], pj_use("M.Y1", i - 1))
                dve.wait_ge(pj_free[pj_bank(f"M.H{m}")], pj_use(f"M.H{m}", i))
                nc.vector.tensor_copy(h_hi[:, 2 * m:2 * m + 2, :], g[:, m, :, :]).then_inc(h_hi_done, 1)

            run(dve, body, 0, LAST)

        @block.gpsimd
        def _(pool):
            nc.gpsimd.memset(eps[:, :], EPS)
            nc.gpsimd.memset(half[:, :], -0.5).then_inc(exponents_set, 1)
            pool.wait_ge(exponents_set, 1)

            def rstds(l, i, stage):
                n, u = LN[l], unit(stage, i)
                pool.wait_ge(ln_mv[l], u + 1)
                nc.gpsimd.tensor_tensor(veps[:, n, :], mv[:, n, :, 1], eps[:, :], ALU.add).then_inc(ln_eps[l], 1)
                pool.wait_ge(ln_eps[l], u + 1)
                nc.gpsimd.tensor_tensor(rstd[:, n, :], veps[:, n, :], half[:, :], ALU.pow).then_inc(ln_rstd[l], 1)

            def residual(stage, src, k, u):
                nc.gpsimd.tensor_tensor(xb[stage][:, :, :], src[:, :, :],
                                        brow[:, k, :].unsqueeze(1).broadcast_to([P, T, H]),
                                        ALU.add).then_inc(xb_done[stage], 1)

            def add_offset(a, i):
                u = unit(a, i)
                for r in range(R):
                    pool.wait_ge(masked[a], R * u + r + 1)
                    p3 = prob[a][:, r, :, :]
                    nc.gpsimd.tensor_tensor(p3, p3, of_tile(maskA_off if a == "A" else maskB_off, a, r),
                                            ALU.add).then_inc(offset[a], 1)

            def shift(a, i):
                u = unit(a, i)
                for r in range(R):
                    pool.wait_ge(maxed[a], R * u + r + 1)
                    p3 = prob[a][:, r, :, :].rearrange("p n (b k) -> p (n b) k", b=TILE)
                    nc.gpsimd.tensor_tensor(p3, p3, rmax[a][:, r, :].unsqueeze(2).broadcast_to(
                        [P, BL * TILE, S]), ALU.subtract).then_inc(shifted[a], 1)

            def low_h(m, i):
                u = unit("M", i)
                pool.wait_ge(h_hi_done, GELU * u + m + 1)
                nc.gpsimd.tensor_tensor(h_lo[:, 2 * m:2 * m + 2, :], g[:, m, :, :],
                                        h_hi[:, 2 * m:2 * m + 2, :].bitcast(F32), ALU.subtract).then_inc(h_lo_done, 1)

            def body(i):
                if starts("A", i):
                    pool.wait_ge(rest_in, REST)
                    pool.wait_ge(masks_done, 2)
                if active("B", i):
                    rstds("B", i, "B")
                    residual("B", x1, 1, unit("B", i))
                if active("A", i):
                    residual("A", x_in, 0, unit("A", i))
                if active("C", i):
                    shift("C", i)
                if active("M", i):
                    rstds("C", i, "M")
                if active("B", i):
                    pool.wait_ge(maskb_off_s, unit("B", i) + 1)
                    add_offset("B", i)
                if active("P", i):
                    rstds("A", i, "P")
                if active("B", i):
                    shift("B", i)
                if active("M", i):
                    for m in range(GELU):
                        low_h(m, i)
                if active("A", i):
                    add_offset("A", i)
                    shift("A", i)
                if active("B", i):
                    rstds("M", i, "B")
                    if active("M", i):
                        pool.wait_ge(tokens["M"], T * (unit("M", i) + 1))
                    residual("M", x2, 2, unit("B", i))

            run(pool, body, 0, LAST)


CONST_COLS = [P, 4, 8 * KC, 24]
REST = 16 * (1 + 2 + 1)


def kernel(**inputs):
    import numpy as np
    import concourse.bacc as bacc
    from concourse.bass_utils import run_bass_kernel_spmd

    a = {k: np.asarray(v) for k, v in inputs.items()}
    L0, L1 = "L0_xattn_", "L1_xattn_"

    def by_parity(w):
        v = w.reshape(KC, HALVES, 2, 2, HD, *w.shape[1:])
        return v.transpose(3, 1, 0, 2, 4, *range(5, v.ndim)).reshape(w.shape)

    def columns(vectors):
        return np.concatenate(vectors).reshape(-1, P).T

    feature = np.arange(P)
    arrays = {
        "x": a["x"], "ctx_2048": a["ctx_2048"], "mask_1x1xSxS2_fc1": a["mask_1x1xSxS2_fc1"],
        "mask_Bx1xSxS2_ff1": a["mask_Bx1xSxS2_ff1"], "mask_BxS2_bf1": a["mask_BxS2_bf1"],
        "constants": np.concatenate([
            np.eye(P, dtype=np.float32),
            np.stack([feature // n % 2 == e for n in (HD, 2 * HD) for e in range(2)], 1).astype(np.float32),
            columns([a[L0 + "ln1_s"], a[L0 + "ln1_b"], a[L0 + "ln2_s"], a[L0 + "ln2_b"],
                     a[L0 + "ln3_s"], a[L0 + "ln3_b"], a[L1 + "ln_gamma"], a[L1 + "ln_beta"]]),
            columns([a[L0 + "b_qkv"][:2 * H], by_parity(a[L0 + "b_qkv"][2 * H:]), a[L0 + "b_q"],
                     a[L0 + "b1"], np.zeros(2 * H, np.float32),
                     a[L0 + "b_kv"][:H], by_parity(a[L0 + "b_kv"][H:])])], 1),
        "rows": np.concatenate([a[L0 + "b_ao"], a[L0 + "b_co"], a[L0 + "b2"]])[None],
        "w_A_qkv": np.concatenate([a[L0 + "w_qkv"][:, :2 * H], by_parity(a[L0 + "w_qkv"][:, 2 * H:].T).T], 1),
        "w_A_o": by_parity(a[L0 + "w_ao"]),
        "w_B_q": a[L0 + "w_q"],
        "w_B_kv": np.concatenate([a[L0 + "w_kv"][:, :H], by_parity(a[L0 + "w_kv"][:, H:].T).T], 1),
        "w_B_o": by_parity(a[L0 + "w_co"]),
        "w_M_1": a[L0 + "w1"], "w_M_2": a[L0 + "w2"],
        "w_C_q": a[L1 + "Wq"].T, "w_C_k": a[L1 + "Wk"].T, "w_C_v": by_parity(a[L1 + "Wv"]).T,
        "w_C_o": by_parity(a[L1 + "Wo"].T),
    }
    arrays[L1 + "gate"] = a[L1 + "gate"]
    nc = bacc.Bacc("TRN2", target_bir_lowering=False, num_devices=1)
    arrays = {k: np.ascontiguousarray(v) for k, v in arrays.items()}
    d = {k: nc.dram_tensor("in_" + k, v.shape, mybir.dt.from_np(v.dtype), kind="ExternalInput").ap()
         for k, v in arrays.items()}
    out = nc.dram_tensor("out", (NB, S, H), F32, kind="ExternalOutput").ap()
    build(nc, d, out)
    r = run_bass_kernel_spmd(nc, [{"in_" + k: v for k, v in arrays.items()}], core_ids=[0])
    return r.results[0]["out"]
```
